# Optimizing a Trainium2 kernel written in Bass

```python
import numpy as np
import jax
import jax.numpy as jnp

def _softmax(x, axis=-1):
    return jax.nn.softmax(x, axis=axis)

def _gelu(x):
    return jax.nn.gelu(x, approximate=True)

def _silu(x):
    return jax.nn.silu(x)

def _sigmoid(x):
    return jax.nn.sigmoid(x)

def _layernorm(x, axis=-1, eps=1e-05):
    m = jnp.mean(x, axis=axis, keepdims=True)
    v = jnp.var(x, axis=axis, keepdims=True)
    return (x - m) / jnp.sqrt(v + eps)

def _scatter_add(tgt, idx, src, axis=0):
    return tgt.at[idx].add(src)

def _segment_sum(src, seg, n):
    return jax.ops.segment_sum(src, seg, n)
kernel_name = 'mk_perceiver_d1_seqx_r2_b8b0c0'

def setup_inputs(seed: int=0):
    np.random.seed(seed)
    _w = jnp.asarray

    def _rec_inputs():
        import jax
        import jax.numpy as jnp
        _rk = jax.random.key(seed)
        x = 7.22e-05 + 1 * jax.random.normal(jax.random.fold_in(_rk, 1), (32, 32, 512), jnp.float32)
        _lenS = 32 - jax.random.randint(jax.random.fold_in(_rk, 7), (32,), 0, max(1, 32 // 4) + 1, jnp.int32)
        _lenS2 = 257 - jax.random.randint(jax.random.fold_in(_rk, 8), (32,), 0, max(1, 257 // 4) + 1, jnp.int32)
        _ctx_1024P = jax.random.normal(jax.random.fold_in(_rk, 11), (32, 16, 512), jnp.float32)
        _ctx_1024c = jax.random.dirichlet(jax.random.fold_in(_rk, 511), 0.3 * jnp.ones((16,), jnp.float32), (32, 257))
        _ctx_1024t = jnp.einsum('bsk,bkd->bsd', _ctx_1024c, _ctx_1024P)
        _ctx_1024t = _ctx_1024t * jax.lax.rsqrt(jnp.mean(jnp.square(_ctx_1024t)) + 1e-12) * 0.953939
        ctx_1024 = 4.13588e-05 + 0.999923 * (_ctx_1024t + 0.3 * jax.random.normal(jax.random.fold_in(_rk, 611), (32, 257, 512), jnp.float32))
        return (x, ctx_1024)
    x, ctx_1024 = _rec_inputs()

    def _L0_xattn_setup():
        import jax, jax.numpy as jnp
        import numpy as np
        NUM_HEADS = 16

        def _split_heads(x):
            B, S, D = x.shape
            return x.reshape(B, S, NUM_HEADS, D // NUM_HEADS).transpose(0, 2, 1, 3)
        key = jax.random.key(seed)
        kq, kk, kv = jax.random.split(key, 3)
        B, S, D = (4, 1024, 512)
        return {'queries': jax.random.normal(kq, (B, S, D), dtype=jnp.float32), 'keys': jax.random.normal(kk, (B, S, D), dtype=jnp.float32), 'values': jax.random.normal(kv, (B, S, D), dtype=jnp.float32)}
    _L0_xattn_all = _L0_xattn_setup()
    _L0_xattn_in = {k: v for k, v in _L0_xattn_all.items() if k in ()}
    del _L0_xattn_all

    def _L0_attn_setup():
        import jax, jax.numpy as jnp
        import numpy as np
        NUM_HEADS = 16
        PAD_ID = 0.0
        key = jax.random.key(seed)
        ks = jax.random.split(key, 9)
        B, T, C = (2, 1024, 512)
        x = jax.random.normal(ks[0], (B, T, C), dtype=jnp.float32)
        lim = (6.0 / (C + C)) ** 0.5

        def w(k):
            return jax.random.uniform(k, (C, C), dtype=jnp.float32, minval=-lim, maxval=lim)

        def b(k):
            return jax.random.uniform(k, (C,), dtype=jnp.float32)
        return {'x': x, 'wq_w': w(ks[1]), 'wq_b': b(ks[2]), 'wk_w': w(ks[3]), 'wk_b': b(ks[4]), 'wv_w': w(ks[5]), 'wv_b': b(ks[6]), 'wo_w': w(ks[7]), 'wo_b': b(ks[8])}
    _L0_attn_all = _L0_attn_setup()
    _L0_attn_in = {k: v for k, v in _L0_attn_all.items() if k in ('wq_w', 'wq_b', 'wk_w', 'wk_b', 'wv_w', 'wv_b', 'wo_w', 'wo_b')}
    del _L0_attn_all

    def _L0_ffn_setup():
        import jax, jax.numpy as jnp
        import numpy as np
        TOPK = 8
        NUM_EXPERTS = 64
        FFN = 1536
        CAPACITY = 160

        def _swiglu(x, w1, w2):
            h = x @ w1.T
            x1, x2 = jnp.split(h, 2, axis=-1)
            return x1 * jax.nn.silu(x2) @ w2.T
        key = jax.random.key(seed)
        ks = jax.random.split(key, 6)
        B, S, H = (1, 256, 512)
        scale = 0.02
        return {'hidden_states': jax.random.normal(ks[0], (B, S, H), jnp.float32), 'wg': jax.random.normal(ks[1], (NUM_EXPERTS, H), jnp.float32) * scale, 'shared_w1': jax.random.normal(ks[2], (2 * FFN, H), jnp.float32) * scale, 'shared_w2': jax.random.normal(ks[3], (H, FFN), jnp.float32) * scale, 'expert_w1': jax.random.normal(ks[4], (NUM_EXPERTS, 2 * FFN, H), jnp.float32) * scale, 'expert_w2': jax.random.normal(ks[5], (NUM_EXPERTS, H, FFN), jnp.float32) * scale}
    _L0_ffn_all = _L0_ffn_setup()
    _L0_ffn_in = {k: v for k, v in _L0_ffn_all.items() if k in ('wg', 'shared_w1', 'shared_w2', 'expert_w1', 'expert_w2')}
    del _L0_ffn_all
    return {'x': x, 'ctx_1024': ctx_1024, 'L0_attn_wq_w': _L0_attn_in['wq_w'], 'L0_attn_wq_b': _L0_attn_in['wq_b'], 'L0_attn_wk_w': _L0_attn_in['wk_w'], 'L0_attn_wk_b': _L0_attn_in['wk_b'], 'L0_attn_wv_w': _L0_attn_in['wv_w'], 'L0_attn_wv_b': _L0_attn_in['wv_b'], 'L0_attn_wo_w': _L0_attn_in['wo_w'], 'L0_attn_wo_b': _L0_attn_in['wo_b'], 'L0_ffn_wg': _L0_ffn_in['wg'], 'L0_ffn_shared_w1': _L0_ffn_in['shared_w1'], 'L0_ffn_shared_w2': _L0_ffn_in['shared_w2'], 'L0_ffn_expert_w1': _L0_ffn_in['expert_w1'], 'L0_ffn_expert_w2': _L0_ffn_in['expert_w2']}

def reference(x, ctx_1024, L0_attn_wq_w, L0_attn_wq_b, L0_attn_wk_w, L0_attn_wk_b, L0_attn_wv_w, L0_attn_wv_b, L0_attn_wo_w, L0_attn_wo_b, L0_ffn_wg, L0_ffn_shared_w1, L0_ffn_shared_w2, L0_ffn_expert_w1, L0_ffn_expert_w2):
    import jax
    import jax.numpy as jnp

    def _L0_xattn_ref(queries, keys, values):
        import jax, jax.numpy as jnp
        import numpy as np
        NUM_HEADS = 16

        def _split_heads(x):
            B, S, D = x.shape
            return x.reshape(B, S, NUM_HEADS, D // NUM_HEADS).transpose(0, 2, 1, 3)
        q = _split_heads(queries)
        k = _split_heads(keys)
        v = _split_heads(values)
        d_k = k.shape[-1]
        scale = 1.0 / jnp.sqrt(jnp.asarray(d_k, dtype=q.dtype))
        scores = jnp.einsum('bhqd,bhkd->bhqk', q, k) * scale
        weights = jax.nn.softmax(scores, axis=-1)
        out = jnp.einsum('bhqk,bhkd->bhqd', weights, v)
        B, H, S, Dh = out.shape
        return out.transpose(0, 2, 1, 3).reshape(B, S, H * Dh)

    def _L0_attn_ref(x, wq_w, wq_b, wk_w, wk_b, wv_w, wv_b, wo_w, wo_b):
        import jax, jax.numpy as jnp
        import numpy as np
        NUM_HEADS = 16
        PAD_ID = 0.0
        B, T, C = x.shape
        H = NUM_HEADS
        Dh = C // H
        scale = Dh ** (-0.5)
        q = (x @ wq_w.T + wq_b).reshape(B, T, H, Dh)
        k = (x @ wk_w.T + wk_b).reshape(B, T, H, Dh)
        v = (x @ wv_w.T + wv_b).reshape(B, T, H, Dh)
        scores = jnp.einsum('bthd,bshd->bhts', q, k) * scale
        key_mask = (x[:, :, 0] != PAD_ID)[:, None, None, :]
        scores = jnp.where(key_mask, scores, -jnp.inf)
        attn = jax.nn.softmax(scores, axis=-1)
        out = jnp.einsum('bhts,bshd->bthd', attn, v).reshape(B, T, C)
        return out @ wo_w.T + wo_b

    def _L0_ffn_ref(hidden_states, wg, shared_w1, shared_w2, expert_w1, expert_w2):
        import jax, jax.numpy as jnp
        import numpy as np
        TOPK = 8
        NUM_EXPERTS = 64
        FFN = 1536
        CAPACITY = 160

        def _swiglu(x, w1, w2):
            h = x @ w1.T
            x1, x2 = jnp.split(h, 2, axis=-1)
            return x1 * jax.nn.silu(x2) @ w2.T
        B, S, H = hidden_states.shape
        T = B * S
        x = hidden_states.reshape(T, H)
        shared_out = _swiglu(x, shared_w1, shared_w2)
        logits = x.astype(jnp.float32) @ wg.T
        gates = jax.nn.softmax(logits, axis=-1)
        w_topk, idx_topk = jax.lax.top_k(gates, TOPK)
        denom = jnp.maximum(w_topk.sum(-1, keepdims=True), jnp.finfo(jnp.float32).eps)
        w_topk = w_topk / denom
        A = T * TOPK
        flat_e = idx_topk.reshape(A)
        flat_w = w_topk.reshape(A)
        flat_t = jnp.repeat(jnp.arange(T), TOPK)
        order = jnp.argsort(flat_e)
        se, st, sw = (flat_e[order], flat_t[order], flat_w[order])
        counts = jnp.zeros(NUM_EXPERTS, jnp.int32).at[flat_e].add(1)
        starts = jnp.cumsum(counts) - counts
        rank = jnp.arange(A) - starts[se]
        valid = rank < CAPACITY
        buf = jnp.zeros((NUM_EXPERTS, CAPACITY, H), x.dtype).at[se, rank].set(x[st], mode='drop')
        h = jnp.einsum('ech,efh->ecf', buf, expert_w1)
        x1, x2 = jnp.split(h, 2, axis=-1)
        out = jnp.einsum('ecf,ehf->ech', x1 * jax.nn.silu(x2), expert_w2)
        y = out[se, jnp.clip(rank, 0, CAPACITY - 1)]
        y = jnp.where(valid[:, None], y * sw[:, None].astype(y.dtype), 0.0)
        combined = jnp.zeros((T, H), x.dtype).at[st].add(y)
        return (shared_out + combined).reshape(B, S, H)
    x = x + _L0_xattn_ref(_layernorm(x, axis=-1), ctx_1024, ctx_1024)
    x = x + _L0_attn_ref(_layernorm(x, axis=-1), L0_attn_wq_w, L0_attn_wq_b, L0_attn_wk_w, L0_attn_wk_b, L0_attn_wv_w, L0_attn_wv_b, L0_attn_wo_w, L0_attn_wo_b)
    x = x + _L0_ffn_ref(_layernorm(x, axis=-1), L0_ffn_wg, L0_ffn_shared_w1, L0_ffn_shared_w2, L0_ffn_expert_w1, L0_ffn_expert_w2)
    return x

_drawn_inputs = setup_inputs


def setup_inputs(seed=0):
    import zlib

    import numpy as np

    out = dict(_drawn_inputs(seed))
    spreads = {}
    factors = {'L0_attn_wk_b': 8.0,
     'L0_ffn_wg': 3.093,
     'L0_ffn_expert_w1': 2.722,
     'L0_ffn_expert_w2': 2.721}
    for name, (base, spread) in spreads.items():
        noise = np.random.default_rng([zlib.crc32(name.encode()), seed]).standard_normal(out[name].shape)
        drawn = base * np.exp(spread * noise) if base else spread * noise
        out[name] = jnp.asarray(drawn.astype(out[name].dtype))
    for name, factor in factors.items():
        out[name] = (out[name] * factor).astype(out[name].dtype)
    return out
```

```python
from contextlib import ExitStack

import concourse.bass as bass
from concourse import mybir

F32 = mybir.dt.float32
F32R = mybir.dt.float32r
BF16 = mybir.dt.bfloat16
I32 = mybir.dt.int32
ALU = mybir.AluOpType
ACT = mybir.ActivationFunctionType
AX = mybir.AxisListType

P = 128
B = 32
SQ = 32
SK = 257
D = 512
G = D // P
DH = 32
T = B * SQ
TT = T // P
NE = 64
TOPK = 8
FFN = 1536
J = FFN // P
CAP = 160
CAP2 = CAP - P
CW = 2 * G * P + D
RAW = 6
HL = 6
AHEAD = 3
LAG = 2
HALF = T // 2
SCALE = float(DH) ** -0.5
EPS = 1e-5
FEPS = 1.1920928955078125e-07
MASKED = -(2.0 ** 126)


class Tally:

    def __init__(self, eng, sem):
        self.eng, self.sem, self.n = eng, sem, 0

    def did(self, ins):
        ins.then_inc(self.sem, 1)
        self.n += 1

    def settle(self):
        self.eng.wait_ge(self.sem, self.n)

    def then(self, ins):
        self.did(ins)
        self.settle()


def layernorm(dve, X, XN, stats, mv, small, done, std_ready, xn_ready):
    for t in range(TT):
        done.did(dve.bn_stats(stats[:, t, :], X[:, t, :]))
    done.settle()
    for t in range(TT):
        done.did(dve.bn_aggr(mv[:, t, :], stats[:, t, :]))
    done.settle()
    var, r, a = small[:, 0, :], small[:, 1, :], small[:, 2, :]
    done.then(dve.tensor_scalar(var, mv[:, :, 1], EPS, None, ALU.add))
    dve.wait_ge(std_ready, 1)
    done.then(dve.reciprocal(r, r))
    done.then(dve.tensor_tensor(a, r, r, ALU.mult))
    done.then(dve.tensor_tensor(a, a, var, ALU.mult))
    done.then(dve.tensor_scalar(a, a, -0.5, 1.5, ALU.mult, ALU.add))
    done.then(dve.tensor_tensor(r, r, a, ALU.mult))
    for t in range(TT):
        dve.tensor_scalar(XN[:, t, :], X[:, t, :], mv[:, t, 0:1], r[:, t:t + 1],
                          ALU.subtract, ALU.mult).then_inc(xn_ready, 1)


def transpose_tiles(pe, ps, XN, ident, xn_ready, xt_psum, xt_copied):
    for t in range(TT):
        pe.wait_ge(xn_ready, t + 1)
        if t >= 2:
            pe.wait_ge(xt_copied, t - 1)
        for g in range(G):
            last = pe.transpose(ps[:, t % 2, g * P:(g + 1) * P], XN[:, t, g * P:(g + 1) * P], ident[:, :])
        last.then_inc(xt_psum, 1)


def copy_tiles(act, ps, XT, small, ln_done, std_ready, xt_psum, xt_copied):
    act.wait_ge(ln_done, 2 * TT + 1)
    act.activation(small[:, 1, :], small[:, 0, :], ACT.Sqrt).then_inc(std_ready, 1)
    for t in range(TT):
        act.wait_ge(xt_psum, t + 1)
        act.activation(XT[:, :, t * P:(t + 1) * P], ps[:, t % 2, :].rearrange("p (g n) -> p g n", g=G),
                       ACT.Copy).then_inc(xt_copied, 1)


def program(nc, x, ctx_k, ctx_v, wq, wk, wv, wo, bq, bk, bv, bo, wg, shared, experts, out, NEXP=NE):
    root = ExitStack()
    with root:
        def allocator(stack):
            def sb(name, shape, dt=F32):
                return stack.enter_context(nc.sbuf_tensor(name, shape, dt))
            return sb

        def sem(name):
            return root.enter_context(nc.semaphore(name))

        sb = allocator(root)
        ps = root.enter_context(nc.psum_tensor("ps", [P, 8, 512], F32))
        xn_dram = nc.dram_tensor("xn_scratch", [T, D], F32, kind="Internal").ap()

        X = sb("X", [P, TT, D])
        ident = sb("ident", [P, P])
        stats = sb("stats", [P, TT, 6])
        mv = sb("mv", [P, TT, 2])
        small = sb("small", [P, 3, TT])
        x_dram = x.rearrange("b s d -> (b s) d").rearrange("(t p) d -> p t d", p=P)
        out_tiles = out[0:T, :].rearrange("(t p) d -> p t d", p=P)

        with ExitStack() as st:
            sb = allocator(st)
            XN = sb("a_XN", [P, TT, D])
            XT = sb("a_XT", [P, G, T])
            Q = sb("a_Q", [P, 4, G, P])
            K = sb("a_K", [P, 4, G, SK])
            V = sb("a_V", [P, 4, 3, D])
            PR = sb("a_PR", [P, 2, G, SK])
            PTa = sb("a_PTa", [P, 2, 2, G, P])
            PTb = sb("a_PTb", [1, 2, G, P])
            AT = sb("a_AT", [P, G, T])
            mx = sb("a_mx", [P, 2, G])
            nm = sb("a_nm", [P, 2, G])
            sm = sb("a_sm", [P, 2, G])
            rs = sb("a_rs", [P, 2, G])

            x_in = sem("a_x_in")
            k_in = [sem(f"a_k_in{i}") for i in range(4)]
            v_in = [sem(f"a_v_in{i}") for i in range(4)]
            ln_done = sem("a_ln_done")
            std_ready = sem("a_std_ready")
            xn_ready = sem("a_xn_ready")
            xt_psum = sem("a_xt_psum")
            xt_copied = sem("a_xt_copied")
            made = sem("a_made")
            zeroed = sem("a_zeroed")
            ident_ready = sem("a_ident_ready")
            q_ready = sem("a_q_ready")
            s_done = sem("a_s_done")
            max_done = sem("a_max_done")
            nm_done = sem("a_nm_done")
            exp_done = sem("a_exp_done")
            rec_done = sem("a_rec_done")
            pr_ready = sem("a_pr_ready")
            t_done = sem("a_t_done")
            pt_ready = sem("a_pt_ready")
            pv_done = sem("a_pv_done")
            at_ready = sem("a_at_ready")
            back_psum = sem("a_back_psum")
            x1_ready = sem("a_x1_ready")

            block = st.enter_context(nc.Block())

            @block.sync
            def _(sp):
                sp.dma_start(X[:, :, :], x_dram).then_inc(x_in, 16)

                def load(q, first):
                    for i in range(4):
                        b = 4 * q + i
                        if not first:
                            sp.wait_ge(s_done, b - 3)
                        sp.dma_start(K[:, i, :, :], ctx_k[b]).then_inc(k_in[i], 16)
                        if not first:
                            sp.wait_ge(pv_done, b - 3)
                        sp.dma_start(V[:, i, 0:2, :], ctx_v[b, 0:2 * P, :].rearrange("(k p) d -> p k d", p=P)).then_inc(v_in[i], 16)
                        sp.dma_start(V[0:1, i, 2, :], ctx_v[b, 2 * P:SK, :]).then_inc(v_in[i], 16)

                load(0, True)
                with sp.Fori(1, TT) as q:
                    load(q, False)

            @block.gpsimd
            def _(pool):
                pool.memset(ident[:, :], 0.0).then_inc(made, 1)
                pool.memset(Q[:, :, :, :], 0.0).then_inc(zeroed, 1)
                pool.wait_ge(made, 1)
                pool.affine_select(out=ident[:, :], in_=ident[:, :], compare_op=ALU.not_equal, fill=1.0, base=0,
                                   pattern=[[-1, P]], channel_multiplier=1).then_inc(ident_ready, 1)
                pool.wait_ge(zeroed, 1)

                def queries(q, first):
                    pool.wait_ge(xt_copied, q + 1)
                    for i in range(4):
                        b = 4 * q + i
                        if not first:
                            pool.wait_ge(s_done, b - 3)
                        for h in range(4):
                            r = slice(32 * h, 32 * h + 32)
                            pool.tensor_copy(Q[r, i, :, r], XT[r, :, bass.ds(P * q + SQ * i, SQ)]).then_inc(q_ready, 1)

                queries(0, True)
                with pool.Fori(1, TT) as q:
                    queries(q, False)

            @block.tensor
            def _(pe):
                pe.wait_ge(ident_ready, 1)
                transpose_tiles(pe, ps, XN, ident, xn_ready, xt_psum, xt_copied)
                pe.wait_ge(xt_copied, TT)

                def scores(b, i, q, first):
                    pe.wait_ge(q_ready, 4 * b + 4)
                    pe.wait_ge(k_in[i], 16 * q + 16)
                    if not (first and i == 0):
                        pe.wait_ge(exp_done, 4 * b)
                    for g in range(G):
                        last = pe.matmul(ps[:, g, 0:SK], Q[:, i, g, :], K[:, i, g, :], start=True, stop=True)
                    last.then_inc(s_done, 1)

                def turn(b, i):
                    pe.wait_ge(pr_ready, b + 1)
                    for g in range(G):
                        for k in range(2):
                            pe.transpose(ps[:, 4 + k, g * P:(g + 1) * P], PR[:, i % 2, g, k * P:(k + 1) * P], ident[:, :])
                        last = pe.transpose(ps[0:1, 6, g * P:(g + 1) * P], PR[:, i % 2, g, 2 * P:SK], ident[:, :])
                    last.then_inc(t_done, 1)

                def values(b, i, vcount):
                    pe.wait_ge(pt_ready, 2 * b + 2)
                    pe.wait_ge(v_in[i], vcount)
                    for g in range(G):
                        w = slice(g * P, (g + 1) * P)
                        for k in range(2):
                            pe.matmul(ps[:, 7, w], V[:, i, k, w], PTa[:, i % 2, k, g, :], start=(k == 0), stop=False)
                        last = pe.matmul(ps[:, 7, w], V[0:1, i, 2, w], PTb[0:1, i % 2, g, :], start=False, stop=True)
                    last.then_inc(pv_done, 1)

                def quad(q, first):
                    for i in range(4):
                        b = 4 * q + i
                        scores(b, i, q, first)
                        if not (first and i < 2):
                            if not (first and i < 3):
                                pe.wait_ge(at_ready, 4 * b - 8)
                            values(b - 2, (i - 2) % 4, 32 * q + 32 * (i >= 2))
                        if not (first and i < 1):
                            turn(b - 1, (i - 1) % 4)

                quad(0, True)
                with pe.Fori(1, TT) as q:
                    quad(q, False)
                pe.wait_ge(at_ready, 4 * (B - 2))
                values(B - 2, 2, 32 * TT)
                turn(B - 1, 3)
                pe.wait_ge(at_ready, 4 * (B - 1))
                values(B - 1, 3, 32 * TT)
                pe.wait_ge(at_ready, 4 * B)
                for t in range(TT):
                    if t >= 2:
                        pe.wait_ge(x1_ready, t - 1)
                    for g in range(G):
                        last = pe.transpose(ps[:, t % 2, g * P:(g + 1) * P], AT[:, g, t * P:(t + 1) * P], ident[:, :])
                    last.then_inc(back_psum, 1)

            @block.scalar
            def _(act):
                copy_tiles(act, ps, XT, small, ln_done, std_ready, xt_psum, xt_copied)

                def copy_pt(b, i):
                    act.wait_ge(t_done, b + 1)
                    act.activation(PTa[:, i % 2, :, :, :].rearrange("p k g n -> p (k g n)"),
                                   ps[:, 4:6, :].rearrange("p k n -> p (k n)"), ACT.Copy).then_inc(pt_ready, 1)
                    act.activation(PTb[0:1, i % 2, :, :].rearrange("p g n -> p (g n)"), ps[0:1, 6, :],
                                   ACT.Copy).then_inc(pt_ready, 1)

                def quad(q, first):
                    for i in range(4):
                        b = 4 * q + i
                        act.wait_ge(nm_done, b + 1)
                        if not (first and i < 2):
                            act.wait_ge(t_done, b - 1)
                        for g in range(G):
                            act.activation(PR[:, i % 2, g, :], ps[:, g, 0:SK], ACT.Exp, bias=nm[:, i % 2, g:g + 1],
                                           scale=SCALE, accum_out=sm[:, i % 2, g:g + 1]).then_inc(exp_done, 1)
                        if not (first and i < 1):
                            if not (first and i < 3):
                                act.wait_ge(pv_done, b - 2)
                            copy_pt(b - 1, (i - 1) % 4)

                quad(0, True)
                with act.Fori(1, TT) as q:
                    quad(q, False)
                act.wait_ge(pv_done, B - 2)
                copy_pt(B - 1, 3)

            @block.vector
            def _(dve):
                dve.wait_ge(x_in, 16)
                layernorm(dve, X, XN, stats, mv, small, Tally(dve, ln_done), std_ready, xn_ready)

                def diagonal(b, q, i):
                    dve.wait_ge(pv_done, b + 1)
                    for h in range(4):
                        r = slice(32 * h, 32 * h + 32)
                        dve.tensor_copy(AT[r, :, bass.ds(P * q + SQ * i, SQ)],
                                        ps[r, 7, :].rearrange("p (g n) -> p g n", g=G)[:, :, r]).then_inc(at_ready, 1)

                def quad(q, first):
                    for i in range(4):
                        b = 4 * q + i
                        k = i % 2
                        dve.wait_ge(s_done, b + 1)
                        dve.tensor_reduce(mx[:, k, :], ps[:, 0:G, 0:SK], AX.X, ALU.max).then_inc(max_done, 1)
                        dve.wait_ge(max_done, b + 1)
                        if not (first and i < 2):
                            dve.wait_ge(exp_done, 4 * b - 4)
                        dve.tensor_scalar(nm[:, k, :], mx[:, k, :], -SCALE, None, ALU.mult).then_inc(nm_done, 1)
                        if not (first and i < 2):
                            if i < 2:
                                diagonal(b - 2, q - 1, i + 2)
                            else:
                                diagonal(b - 2, q, i - 2)
                        dve.wait_ge(exp_done, 4 * b + 4)
                        dve.reciprocal(rs[:, k, :], sm[:, k, :]).then_inc(rec_done, 1)
                        dve.wait_ge(rec_done, b + 1)
                        dve.tensor_tensor(PR[:, k, :, :], PR[:, k, :, :], rs[:, k, :].rearrange("p (g o) -> p g o", o=1).to_broadcast([P, G, SK]),
                                          ALU.mult).then_inc(pr_ready, 1)

                quad(0, True)
                with dve.Fori(1, TT) as q:
                    quad(q, False)
                diagonal(B - 2, TT - 1, 2)
                diagonal(B - 1, TT - 1, 3)
                for t in range(TT):
                    dve.wait_ge(back_psum, t + 1)
                    dve.tensor_tensor(X[:, t, :], X[:, t, :], ps[:, t % 2, :], ALU.add).then_inc(x1_ready, 1)
                dve.wait_ge(x1_ready, TT)

        with ExitStack() as st:
            sb = allocator(st)
            XN = sb("b_XN", [P, TT, D])
            XT = sb("b_XT", [P, G, T])
            W = sb("b_W", [P, 4, G, D])
            bqk = sb("b_bqk", [P, 2, G])
            bvo = sb("b_bvo", [P, 2, D])
            QT = sb("b_QT", [P, G, T])
            KT = sb("b_KT", [P, G, T])
            VV = sb("b_VV", [P, TT, D])
            Q = sb("b_Q", [P, 2, 4, G, P])
            mask = sb("b_mask", [1, 1, T], BF16)
            ones = sb("b_ones", [1, P], BF16)
            S = sb("b_S", [P, 2, 4 * G, SQ])
            PT = sb("b_PT", [P, 2, G, P])
            AT = sb("b_AT", [P, G, T])
            mx = sb("b_mx", [P, 4 * G])
            sm = sb("b_sm", [P, 4 * G])

            w_in = sem("b_w_in")
            ln_done = sem("b_ln_done")
            std_ready = sem("b_std_ready")
            xn_ready = sem("b_xn_ready")
            xt_psum = sem("b_xt_psum")
            xt_copied = sem("b_xt_copied")
            consts = sem("b_consts")
            mask_ready = sem("b_mask_ready")
            proj_psum = sem("b_proj_psum")
            proj_even = sem("b_proj_even")
            proj_odd = sem("b_proj_odd")
            q_ready = sem("b_q_ready")
            s_done = sem("b_s_done")
            soft = sem("b_soft")
            sub_done = sem("b_sub_done")
            exp_done = sem("b_exp_done")
            pr_ready = sem("b_pr_ready")
            t_done = sem("b_t_done")
            pt_ready = sem("b_pt_ready")
            pv_done = sem("b_pv_done")
            at_ready = sem("b_at_ready")
            o_psum = sem("b_o_psum")
            o_added = sem("b_o_added")
            x2_done = sem("b_x2_done")

            block = st.enter_context(nc.Block())

            @block.sync
            def _(sp):
                for i, w in enumerate((wq, wk, wv, wo)):
                    sp.dma_start(W[:, i, :, :], w).then_inc(w_in, 16)
                for i, v in enumerate((bq, bk)):
                    sp.dma_start(bqk[:, i, :], v).then_inc(w_in, 16)
                for i, v in enumerate((bv, bo)):
                    sp.dma_start(bvo[:, i, :], v.to_broadcast([P, D])).then_inc(w_in, 16)

            @block.gpsimd
            def _(pool):
                pool.memset(Q[:, :, :, :, :], 0.0).then_inc(consts, 1)
                pool.memset(ones[:, :], 1.0).then_inc(consts, 1)
                pool.wait_ge(consts, 2)
                for t in range(TT):
                    pool.wait_ge(proj_even, 4 * (t // 4) + 4)
                    if t >= 2:
                        pool.wait_ge(s_done, t - 1)
                    for h in range(4):
                        r = slice(32 * h, 32 * h + 32)
                        pool.tensor_copy(Q[r, t % 2, :, :, r].rearrange("p b g n -> p g b n"),
                                         QT[r, :, t * P:(t + 1) * P].rearrange("p g (b n) -> p g b n", b=4)).then_inc(q_ready, 1)

            @block.tensor
            def _(pe):
                transpose_tiles(pe, ps, XN, ident, xn_ready, xt_psum, xt_copied)
                pe.wait_ge(xt_copied, TT)
                pe.wait_ge(w_in, 16 * 8)
                n = 0

                def bank():
                    if n >= 4:
                        pe.wait_ge(proj_even if n % 2 == 0 else proj_odd, (n - 4) // 2 + 1)
                    return ps[:, 2 + n % 4, :]

                for half in range(2):
                    cols = slice(half * HALF, half * HALF + HALF)
                    for o in range(G):
                        for i in range(2):
                            dst = bank()
                            for k in range(G):
                                last = pe.matmul(dst, W[:, i, k, o * P:(o + 1) * P], XT[:, k, cols], start=(k == 0), stop=(k == G - 1))
                            last.then_inc(proj_psum, 1)
                            n += 1
                for t in range(TT):
                    dst = bank()
                    for k in range(G):
                        last = pe.matmul(dst, XT[:, k, t * P:(t + 1) * P], W[:, 2, k, :], start=(k == 0), stop=(k == G - 1))
                    last.then_inc(proj_psum, 1)
                    n += 1
                pe.wait_ge(proj_odd, 12)
                pe.wait_ge(proj_even, 12)
                pe.wait_ge(mask_ready, 1)

                def scores(t):
                    pe.wait_ge(q_ready, 4 * t + 4)
                    if t >= 2:
                        pe.wait_ge(sub_done, t - 1)
                    bk_ = ps[:, t % 2, :]
                    pe.matmul(bk_, ones[:, :], mask[0:1, :, t * P:(t + 1) * P].to_broadcast([1, G, P]),
                              start=True, stop=False, skip_group_check=True)
                    for g in range(G):
                        for b in range(4):
                            c = g * P + b * SQ
                            last = pe.matmul(bk_[:, c:c + SQ], Q[:, t % 2, b, g, :], KT[:, g, t * P + b * SQ:t * P + (b + 1) * SQ],
                                             start=False, stop=(g == 3 and b == 3), skip_group_check=True)
                    last.then_inc(s_done, 1)

                def turn(t):
                    pe.wait_ge(pr_ready, t + 1)
                    if t >= 1:
                        pe.wait_ge(pt_ready, t)
                    for g in range(G):
                        last = pe.transpose(ps[:, 2, g * P:(g + 1) * P], S[:, t % 2, 4 * g:4 * g + 4, :].rearrange("p b n -> p (b n)"), ident[:, :])
                    last.then_inc(t_done, 1)

                def values(t):
                    pe.wait_ge(pt_ready, t + 1)
                    if t >= 1:
                        pe.wait_ge(at_ready, 4 * t)
                    for b in range(4):
                        r = slice(32 * b, 32 * b + 32)
                        for g in range(G):
                            last = pe.matmul(ps[:, 4 + b, g * P:(g + 1) * P], VV[r, t, g * P:(g + 1) * P], PT[r, t % 2, g, :],
                                             start=True, stop=True)
                    last.then_inc(pv_done, 1)

                for t in range(TT + 2):
                    if t < TT:
                        scores(t)
                    if t >= 2:
                        values(t - 2)
                    if 1 <= t <= TT:
                        turn(t - 1)
                pe.wait_ge(at_ready, 4 * TT)
                for t in range(TT):
                    if t >= 2:
                        pe.wait_ge(o_added, t - 1)
                    for k in range(G):
                        last = pe.matmul(ps[:, t % 2, :], AT[:, k, t * P:(t + 1) * P], W[:, 3, k, :], start=(k == 0), stop=(k == G - 1))
                    last.then_inc(o_psum, 1)

            @block.scalar
            def _(act):
                copy_tiles(act, ps, XT, small, ln_done, std_ready, xt_psum, xt_copied)
                act.wait_ge(w_in, 16 * 8)
                n = 0
                for half in range(2):
                    for o in range(G):
                        act.wait_ge(proj_psum, n + 1)
                        act.activation(QT[:, o, half * HALF:half * HALF + HALF], ps[:, 2 + n % 4, :], ACT.Identity,
                                       bias=bqk[:, 0, o:o + 1]).then_inc(proj_even, 1)
                        n += 2
                for t in range(0, TT, 2):
                    act.wait_ge(proj_psum, n + 1)
                    act.activation(VV[:, t, :], ps[:, 2 + n % 4, :], ACT.Copy).then_inc(proj_even, 1)
                    n += 2
                for t in range(TT + 1):
                    if t < TT:
                        act.wait_ge(sub_done, t + 1)
                        act.activation(S[:, t % 2, :, :], S[:, t % 2, :, :], ACT.Exp, scale=SCALE).then_inc(exp_done, 1)
                    if t >= 1:
                        act.wait_ge(t_done, t)
                        if t >= 3:
                            act.wait_ge(pv_done, t - 2)
                        act.activation(PT[:, (t - 1) % 2, :, :].rearrange("p g n -> p (g n)"), ps[:, 2, :], ACT.Copy).then_inc(pt_ready, 1)

            @block.vector
            def _(dve):
                layernorm(dve, X, XN, stats, mv, small, Tally(dve, ln_done), std_ready, xn_ready)
                dve.wait_ge(xt_copied, TT)
                dve.tensor_scalar(mask[0:1, 0, :], XT[0:1, 0, :], 0.0, MASKED, ALU.is_equal, ALU.mult).then_inc(mask_ready, 1)
                dve.wait_ge(w_in, 16 * 8)
                n = 1
                for half in range(2):
                    for o in range(G):
                        dve.wait_ge(proj_psum, n + 1)
                        dve.tensor_scalar(KT[:, o, half * HALF:half * HALF + HALF], ps[:, 2 + n % 4, :], bqk[:, 1, o:o + 1], None,
                                          ALU.add).then_inc(proj_odd, 1)
                        n += 2
                for t in range(1, TT, 2):
                    dve.wait_ge(proj_psum, n + 1)
                    dve.tensor_tensor(VV[:, t, :], ps[:, 2 + n % 4, :], bvo[:, 0, :], ALU.add).then_inc(proj_odd, 1)
                    n += 2
                chain = Tally(dve, soft)
                dve.wait_ge(proj_even, 12)
                for t in range(0, TT, 2):
                    chain.did(dve.tensor_tensor(VV[:, t, :], VV[:, t, :], bvo[:, 0, :], ALU.add))
                for t in range(TT):
                    chain.did(dve.tensor_tensor(X[:, t, :], X[:, t, :], bvo[:, 1, :], ALU.add))
                chain.settle()

                def diagonal(t):
                    dve.wait_ge(pv_done, t + 1)
                    for h in range(4):
                        r = slice(32 * h, 32 * h + 32)
                        dve.tensor_copy(AT[r, :, t * P:(t + 1) * P].rearrange("p g (b n) -> p g b n", b=4),
                                        ps[r, 4:8, :].rearrange("p b (g n) -> p g b n", g=G)[:, :, :, r]).then_inc(at_ready, 1)

                for t in range(TT):
                    dve.wait_ge(s_done, t + 1)
                    bk_ = ps[:, t % 2, :].rearrange("p (c n) -> p c n", n=SQ)
                    bc = lambda v: v[:, :].rearrange("p (c o) -> p c o", o=1).to_broadcast([P, 4 * G, SQ])
                    chain.then(dve.tensor_reduce(mx[:, :], bk_, AX.X, ALU.max))
                    if t >= 2:
                        dve.wait_ge(t_done, t - 1)
                    dve.tensor_tensor(S[:, t % 2, :, :], bk_, bc(mx), ALU.subtract).then_inc(sub_done, 1)
                    if t >= 2:
                        diagonal(t - 2)
                    dve.wait_ge(exp_done, t + 1)
                    chain.then(dve.tensor_reduce(sm[:, :], S[:, t % 2, :, :], AX.X, ALU.add))
                    chain.then(dve.reciprocal(sm[:, :], sm[:, :]))
                    dve.tensor_tensor(S[:, t % 2, :, :], S[:, t % 2, :, :], bc(sm), ALU.mult).then_inc(pr_ready, 1)
                    dve.wait_ge(pr_ready, t + 1)
                diagonal(TT - 2)
                diagonal(TT - 1)
                for t in range(TT):
                    dve.wait_ge(o_psum, t + 1)
                    dve.tensor_tensor(X[:, t, :], X[:, t, :], ps[:, t % 2, :], ALU.add).then_inc(o_added, 1)
                dve.wait_ge(o_added, TT)

        sb = allocator(root)
        RK = sb("RK", [P, NE, TT])
        WS = sb("WS", [P, NE, TT, 3], BF16)
        XSh = sb("XSh", [P, G, T], F32R)
        XSl = sb("XSl", [P, G, T], F32R)
        with ExitStack() as st:
            sb = allocator(st)
            XN = sb("c_XN", [P, TT, D])
            XT = sb("c_XT", [P, G, T])
            wgs = sb("c_wg", [P, G, NE])
            L = sb("c_L", [P, TT, NE])
            M = sb("c_M", [P, TT, NE])
            sel = sb("c_sel", [P, TT, NE])
            selb = sb("c_selb", [P, TT, NE], BF16)
            before = sb("c_before", [P, P], BF16)
            ones = sb("c_ones", [P, P], BF16)
            top = sb("c_top", [P, TT, 8])
            red = sb("c_red", [P, 3, TT])
            zero = sb("c_zero", [P, D])

            wg_in = sem("c_wg_in")
            ln_done = sem("c_ln_done")
            std_ready = sem("c_std_ready")
            xn_ready = sem("c_xn_ready")
            xt_psum = sem("c_xt_psum")
            xt_copied = sem("c_xt_copied")
            xs_high = sem("c_xs_high")
            xs_low = sem("c_xs_low")
            consts = sem("c_consts")
            consts2 = sem("c_consts2")
            lg_psum = sem("c_lg_psum")
            shifted = sem("c_shifted")
            exped = sem("c_exped")
            chain_s = sem("c_chain")
            sel_ready = sem("c_sel_ready")
            rk_psum = sem("c_rk_psum")
            scratch_out = sem("c_scratch_out")

            block = st.enter_context(nc.Block())

            @block.sync
            def _(sp):
                sp.dma_start(wgs[:, :, :], wg).then_inc(wg_in, 16)
                sp.wait_ge(xn_ready, TT)
                sp.dma_start(xn_dram.rearrange("(t p) d -> p t d", p=P), XN[:, :, :]).then_inc(scratch_out, 16)
                sp.wait_ge(consts, 3)
                sp.dma_start(out[T:T + P, :], zero[:, :]).then_inc(scratch_out, 16)
                sp.dma_start(out[T + P:T + CAP, :], zero[0:CAP2, :]).then_inc(scratch_out, 16)
                sp.wait_ge(scratch_out, 48)

            @block.gpsimd
            def _(pool):
                pool.memset(before[:, :], 1.0).then_inc(consts, 1)
                pool.memset(ones[:, :], 1.0).then_inc(consts, 1)
                pool.memset(zero[:, :], 0.0).then_inc(consts, 1)
                pool.wait_ge(consts, 3)
                pool.affine_select(out=before[:, :], in_=before[:, :], compare_op=ALU.is_gt, fill=0.0, base=0,
                                   pattern=[[1, P]], channel_multiplier=-1).then_inc(consts2, 1)

            @block.tensor
            def _(pe):
                transpose_tiles(pe, ps, XN, ident, xn_ready, xt_psum, xt_copied)
                pe.wait_ge(xt_copied, TT)
                pe.wait_ge(wg_in, 16)
                for t in range(TT):
                    for k in range(G):
                        last = pe.matmul(ps[:, 2, t * NE:(t + 1) * NE], XT[:, k, t * P:(t + 1) * P], wgs[:, k, :],
                                         start=(k == 0), stop=(k == G - 1))
                last.then_inc(lg_psum, 1)
                pe.wait_ge(consts2, 1)
                pe.wait_ge(sel_ready, 1)
                for t in range(TT):
                    for s in range(t + 1):
                        last = pe.matmul(ps[:, 3, t * NE:(t + 1) * NE], before[:, :] if s == t else ones[:, :], selb[:, s, :],
                                         start=(s == 0), stop=(s == t))
                last.then_inc(rk_psum, 1)

            @block.scalar
            def _(act):
                copy_tiles(act, ps, XT, small, ln_done, std_ready, xt_psum, xt_copied)
                act.wait_ge(xt_copied, TT)
                act.wait_ge(shifted, 1)
                act.activation(L[:, :, :], L[:, :, :], ACT.Exp).then_inc(exped, 1)
                for k in range(G):
                    act.activation(XSh[:, k, :], XT[:, k, :], ACT.Copy).then_inc(xs_high, 1)

            @block.vector
            def _(dve):
                layernorm(dve, X, XN, stats, mv, small, Tally(dve, ln_done), std_ready, xn_ready)
                chain = Tally(dve, chain_s)
                bc = lambda v: v.rearrange("p (t o) -> p t o", o=1).to_broadcast([P, TT, NE])
                dve.wait_ge(lg_psum, 1)
                lg = ps[:, 2, :].rearrange("p (t e) -> p t e", e=NE)
                chain.then(dve.tensor_reduce(red[:, 0, :], lg, AX.X, ALU.max))
                dve.tensor_tensor(L[:, :, :], lg, bc(red[:, 0, :]), ALU.subtract).then_inc(shifted, 1)
                dve.wait_ge(exped, 1)
                chain.then(dve.tensor_reduce(red[:, 1, :], L[:, :, :], AX.X, ALU.add))
                chain.then(dve.reciprocal(red[:, 1, :], red[:, 1, :]))
                chain.then(dve.tensor_tensor(L[:, :, :], L[:, :, :], bc(red[:, 1, :]), ALU.mult))
                for t in range(TT):
                    chain.did(dve.max(top[:, t, :], L[:, t, :]))
                chain.settle()
                for t in range(TT):
                    chain.did(dve.match_replace(M[:, t, :], top[:, t, :], L[:, t, :], -1.0))
                chain.settle()
                chain.then(dve.tensor_scalar(sel[:, :, :], M[:, :, :], 0.0, None, ALU.is_lt))
                dve.tensor_copy(selb[:, :, :], sel[:, :, :]).then_inc(sel_ready, 1)
                chain.did(dve.tensor_reduce(red[:, 2, :], top[:, :, :], AX.X, ALU.add))
                chain.then(dve.tensor_tensor(L[:, :, :], L[:, :, :], sel[:, :, :], ALU.mult))
                chain.then(dve.tensor_scalar(red[:, 2, :], red[:, 2, :], FEPS, None, ALU.max))
                chain.then(dve.reciprocal(red[:, 2, :], red[:, 2, :]))
                chain.then(dve.tensor_tensor(L[:, :, :], L[:, :, :], bc(red[:, 2, :]), ALU.mult))
                for i in range(3):
                    part = WS[:, 0:NE, :, i].rearrange("p e t -> p t e")
                    chain.then(dve.tensor_copy(part, L[:, :, :]))
                    if i < 2:
                        chain.then(dve.tensor_tensor(L[:, :, :], L[:, :, :], part, ALU.subtract))
                dve.wait_ge(rk_psum, 1)
                rk = RK[:, 0:NE, :].rearrange("p e t -> p t e")
                chain.then(dve.scalar_tensor_tensor(rk, ps[:, 3, :].rearrange("p (t e) -> p t e", e=NE), 1.0, sel[:, :, :],
                                                    ALU.add, ALU.mult))
                chain.then(dve.tensor_scalar(RK[:, 0:NE, :], RK[:, 0:NE, :], -1.0, None, ALU.add))
                for k in range(G):
                    dve.wait_ge(xs_high, k + 1)
                    dve.tensor_tensor(XSl[:, k, :], XT[:, k, :], XSh[:, k, :], ALU.subtract).then_inc(xs_low, 1)
                dve.wait_ge(xs_low, G)

        with ExitStack() as st:
            sb = allocator(st)
            raw = sb("d_raw", [P, RAW, CW])
            hi = sb("d_hi", [P, HL, CW], F32R)
            lo = sb("d_lo", [P, HL, CW], F32R)
            SL = sb("d_SL", [P, 2, HALF])
            GF = sb("d_GF", [P, 2, HALF])
            Gh = sb("d_Gh", [P, 3, HALF], F32R)
            Gl = sb("d_Gl", [P, 3, HALF], F32R)
            OT = sb("d_OT", [P, G, HALF])
            iota = sb("d_iota", [P, CAP], BF16)
            tick = sb("d_tick", [P, 1])
            RKe = sb("d_RKe", [P, TT])
            OH = sb("d_OH", [P, TT, CAP], BF16)
            RT = sb("d_RT", [P, TT, 6], BF16)
            LS = sb("d_LS", [P, 2, 6])
            slot = sb("d_slot", [P, 2])
            tk = sb("d_tk", [P, 4, 2])
            gidx = sb("d_gidx", [P, 2], I32)
            sidxn = sb("d_sidxn", [P, 2], I32)
            sidx = sb("d_sidx", [P, 2], I32)
            gaten = sb("d_gaten", [P, 2])
            gate = sb("d_gate", [P, 2])
            XG = sb("d_XG", [P, 2, D])
            XEh = sb("d_XEh", [P, G, CAP], F32R)
            XEl = sb("d_XEl", [P, G, CAP], F32R)
            Y = sb("d_Y", [P, 2, D])

            raw_in = [sem(f"d_raw_in{i}") for i in range(RAW)]
            hi_ready = sem("d_hi_ready")
            lo_ready = sem("d_lo_ready")
            h_psum = sem("d_h_psum")
            silu_done = sem("d_silu_done")
            gf_done = sem("d_gf_done")
            gh_done = sem("d_gh_done")
            gl_done = sem("d_gl_done")
            dn_done = sem("d_dn_done")
            so_copied = sem("d_so_copied")
            so_turned = sem("d_so_turned")
            so_added = sem("d_so_added")
            so_out = sem("d_so_out")
            ls_clear = sem("d_ls_clear")
            consts = sem("d_consts")
            picked = sem("d_picked")
            ticked = sem("d_ticked")
            oh_ready = sem("d_oh_ready")
            ls_psum = sem("d_ls_psum")
            list_s = sem("d_list")
            list_ready = sem("d_list_ready")
            list_kept = sem("d_list_kept")
            gathered = sem("d_gathered")
            xe_psum = sem("d_xe_psum")
            xeh_done = sem("d_xeh_done")
            xel_done = sem("d_xel_done")
            ot_copied = sem("d_ot_copied")
            y_psum = sem("d_y_psum")
            y_ready = sem("d_y_ready")
            added = sem("d_added")

            block = st.enter_context(nc.Block())

            FIRST = 2

            def up_w(buf, j, part, k):
                at = (part * G + k) * P
                return buf[:, j % HL, at:at + P]

            def down_w(buf, j, g):
                at = 2 * G * P + g * P
                return buf[:, j % HL, at:at + P]

            def h_view(j, part, w):
                if w == HALF:
                    return ps[:, 2 * (j % 2) + part, :]
                return ps[:, 2 + j % 2, part * CAP:(part + 1) * CAP]

            def pair(bank):
                return ps[:, bank, 0:2 * CAP].rearrange("p (k n) -> p k n", k=2)

            @block.sync
            def _(sp):
                def load(src, u, j):
                    if not (isinstance(u, int) and J * u + j < RAW):
                        sp.wait_ge(hi_ready, J * u + j - RAW + 1)
                        sp.wait_ge(lo_ready, J * u + j - RAW + 1)
                    sp.dma_start(raw[:, j % RAW, :], src).then_inc(raw_in[j % RAW], 16)

                for half in range(2):
                    for j in range(J):
                        load(shared[j], half, j)
                with sp.Fori(0, NEXP) as e:
                    for j in range(J):
                        load(experts[e, j], FIRST + e, j)

            @block.scalar
            def _(act):
                def split(u, j):
                    n = J * u + j
                    act.wait_ge(raw_in[j % RAW], 16 * (J // RAW * u + j // RAW + 1))
                    if not (isinstance(u, int) and n < HL):
                        act.wait_ge(dn_done, n - HL + 1)
                    act.activation(hi[:, j % HL, :], raw[:, j % RAW, :], ACT.Copy).then_inc(hi_ready, 1)

                def silu(u, j, w):
                    n = J * u + j
                    act.wait_ge(h_psum, n + 1)
                    if not (isinstance(u, int) and n < 2):
                        act.wait_ge(gf_done, n - 1)
                    act.activation(SL[:, j % 2, 0:w], h_view(j, 0, w), ACT.Silu).then_inc(silu_done, 1)

                def high(u, j, w):
                    n = J * u + j
                    act.wait_ge(gf_done, n + 1)
                    if not (isinstance(u, int) and n < 3):
                        act.wait_ge(dn_done, n - 2)
                    act.activation(Gh[:, j % 3, 0:w], GF[:, j % 2, 0:w], ACT.Copy).then_inc(gh_done, 1)

                def tokens(e):
                    act.wait_ge(xe_psum, e + 1)
                    for i in range(2):
                        act.activation(XEh[:, 2 * i:2 * i + 2, :], pair(4 + i), ACT.Copy).then_inc(xeh_done, 1)

                def take_out(e):
                    act.wait_ge(dn_done, J * (FIRST + e) + J)
                    for i in range(2):
                        act.activation(OT[:, 2 * i:2 * i + 2, 0:CAP], pair(i), ACT.Copy).then_inc(ot_copied, 1)

                def weigh(e, first=False):
                    act.wait_ge(y_psum, e + 1)
                    act.wait_ge(list_kept, 2 * e + 2)
                    if not first:
                        act.wait_ge(added, 32 * e)
                    act.activation(Y[:, 0, :], ps[:, 6, :], ACT.Copy, scale=gate[:, 0:1]).then_inc(y_ready, 1)
                    act.activation(Y[0:CAP2, 1, :], ps[0:CAP2, 7, :], ACT.Copy, scale=gate[0:CAP2, 1:2]).then_inc(y_ready, 1)

                def expert(e, last=False):
                    u = FIRST + e
                    if not (isinstance(e, int) and e == 0):
                        take_out(e - 1)
                    for j in range(J):
                        silu(u, j, CAP)
                        if j == 1 and not (isinstance(e, int) and e == 0):
                            weigh(e - 1, isinstance(e, int) and e == 1)
                        if j == J - 1:
                            high(u, j, CAP)
                            if not last:
                                act.wait_ge(h_psum, J * u + J)
                                tokens(e + 1)
                        if not (last and j + AHEAD >= J):
                            split(u, j + AHEAD)
                        if j < J - 1:
                            high(u, j, CAP)

                for n in range(AHEAD):
                    split(0, n)
                for half in range(2):
                    for j in range(J):
                        silu(half, j, HALF)
                        split(half, j + AHEAD)
                        high(half, j, HALF)
                    act.wait_ge(dn_done, half * J + J)
                    for g in range(G):
                        act.activation(OT[:, g, :], ps[:, 4 + g, :], ACT.Copy).then_inc(so_copied, 1)
                tokens(0)
                expert(0)
                expert(1, NEXP == 2)
                if NEXP > 2:
                    if NEXP > 3:
                        with act.Fori(2, NEXP - 1) as e:
                            expert(e)
                    expert(NEXP - 1, True)
                take_out(NEXP - 1)
                weigh(NEXP - 1)

            @block.vector
            def _(dve):
                def split(u, j):
                    n = J * u + j
                    dve.wait_ge(hi_ready, n + 1)
                    dve.tensor_tensor(lo[:, j % HL, :], raw[:, j % RAW, :], hi[:, j % HL, :], ALU.subtract).then_inc(lo_ready, 1)

                def product(u, j, w):
                    n = J * u + j
                    dve.wait_ge(silu_done, n + 1)
                    dve.wait_ge(h_psum, n + 1)
                    if not (isinstance(u, int) and n < 2):
                        dve.wait_ge(gh_done, n - 1)
                        dve.wait_ge(gl_done, n - 1)
                    dve.tensor_tensor(GF[:, j % 2, 0:w], SL[:, j % 2, 0:w], h_view(j, 1, w), ALU.mult).then_inc(gf_done, 1)

                def low(u, j, w):
                    dve.wait_ge(gh_done, J * u + j + 1)
                    dve.tensor_tensor(Gl[:, j % 3, 0:w], GF[:, j % 2, 0:w], Gh[:, j % 3, 0:w], ALU.subtract).then_inc(gl_done, 1)

                def onehot(e, tiles):
                    dve.wait_ge(picked, 2 * e + 2)
                    for t in tiles:
                        dve.tensor_scalar(OH[:, t, :], iota[:, :], RKe[:, t:t + 1], None, ALU.is_equal).then_inc(oh_ready, 1)

                lists = Tally(dve, list_s)
                LIST_STEPS = 7

                def read_list(e):
                    lists.n = LIST_STEPS * e
                    dve.wait_ge(ls_psum, e + 1)
                    lists.did(dve.tensor_copy(LS[:, 0, :], ps[:, 4, 320:326]))
                    lists.did(dve.tensor_copy(LS[0:CAP2, 1, :], ps[0:CAP2, 4, 328:334]))
                    lists.settle()
                    token, a = tk[:, 0, :], tk[:, 1, :]
                    lists.did(dve.tensor_reduce(token, LS[:, :, 0:2], AX.X, ALU.add))
                    lists.did(dve.tensor_reduce(gaten[:, :], LS[:, :, 3:6], AX.X, ALU.add))
                    lists.then(dve.tensor_tensor(a, LS[:, :, 2], slot[:, :], ALU.mult))
                    lists.then(dve.tensor_tensor(a, a, token, ALU.subtract))
                    lists.then(dve.tensor_tensor(a, slot[:, :], a, ALU.subtract))
                    if not (isinstance(e, int) and e == 0):
                        dve.wait_ge(gathered, 32 * e)
                    dve.tensor_copy(sidxn[:, :], a).then_inc(list_ready, 1)
                    dve.tensor_copy(gidx[:, :], token).then_inc(list_ready, 1)
                    dve.wait_ge(list_ready, 2 * e + 2)

                def keep_list(e):
                    if not (isinstance(e, int) and e == 0):
                        dve.wait_ge(added, 32 * e)
                        dve.wait_ge(y_ready, 2 * e)
                    dve.tensor_copy(sidx[:, :], sidxn[:, :]).then_inc(list_kept, 1)
                    dve.tensor_copy(gate[:, :], gaten[:, :]).then_inc(list_kept, 1)
                    dve.wait_ge(list_kept, 2 * e + 2)

                def tokens(e):
                    for i in range(2):
                        dve.wait_ge(xeh_done, 2 * e + i + 1)
                        dve.tensor_tensor(XEl[:, 2 * i:2 * i + 2, :], pair(4 + i), XEh[:, 2 * i:2 * i + 2, :],
                                          ALU.subtract).then_inc(xel_done, 1)

                def expert(e, last=False):
                    u = FIRST + e
                    for j in range(J):
                        product(u, j, CAP)
                        if j == J - 1:
                            low(u, j, CAP)
                            if not last:
                                tokens(e + 1)
                        if not (last and j + AHEAD >= J):
                            split(u, j + AHEAD)
                        if j < J - 1:
                            low(u, j, CAP)
                        if j < 4 and not last:
                            onehot(e + 1, (2 * j, 2 * j + 1))
                        if j == 6:
                            if not (isinstance(e, int) and e == 0):
                                keep_list(e)
                            if not last:
                                read_list(e + 1)

                dve.memset(LS[:, :, :], 0.0).then_inc(ls_clear, 1)
                dve.wait_ge(ls_clear, 1)
                dve.wait_ge(consts, 5)
                onehot(0, range(TT))
                read_list(0)
                keep_list(0)
                for n in range(AHEAD):
                    split(0, n)
                for half in range(2):
                    for j in range(J):
                        product(half, j, HALF)
                        split(half, j + AHEAD)
                        low(half, j, HALF)
                    for t in range(4):
                        dve.wait_ge(so_turned, 4 * half + t + 1)
                        row = 4 * half + t
                        dve.tensor_tensor(X[:, row, :], X[:, row, :], ps[:, t, :], ALU.add).then_inc(so_added, 1)
                tokens(0)
                expert(0)
                expert(1, NEXP == 2)
                if NEXP > 2:
                    if NEXP > 3:
                        with dve.Fori(2, NEXP - 1) as e:
                            expert(e)
                    expert(NEXP - 1, True)

            @block.gpsimd
            def _(pool):
                exact = dict(allow_small_or_imprecise_dtypes=True)
                pool.iota(iota[:, :], [[1, CAP]], base=0, channel_multiplier=0, **exact).then_inc(consts, 1)
                pool.iota(slot[:, :], [[P, 2]], base=T, channel_multiplier=1, **exact).then_inc(consts, 1)
                pool.iota(RT[:, :, 0], [[P, TT]], base=0, channel_multiplier=0, **exact).then_inc(consts, 1)
                pool.iota(RT[:, :, 1], [[0, TT]], base=0, channel_multiplier=1, **exact).then_inc(consts, 1)
                pool.memset(RT[:, :, 2], 1.0).then_inc(consts, 1)
                pool.wait_ge(consts, 5)

                def pick(e):
                    if not (isinstance(e, int) and e == 0):
                        pool.wait_ge(ls_psum, e)
                    pool.tensor_copy(RKe[:, :], RK[:, bass.ds(e, 1), :].rearrange("p o t -> p (o t)")).then_inc(picked, 1)
                    pool.tensor_copy(RT[:, :, 3:6], WS[:, bass.ds(e, 1), :, :].rearrange("p o t c -> p (o t) c")).then_inc(picked, 1)

                def hold(before):
                    if not (isinstance(before, int) and before == 0):
                        pool.wait_ge(ticked, before)
                    pool.tensor_tensor(tick[:, :], iota[:, 0:1], iota[:, 0:1], ALU.add).then_inc(ticked, 1)

                def gather(e):
                    pool.wait_ge(list_ready, 2 * e + 2)
                    if not (isinstance(e, int) and e == 0):
                        pool.wait_ge(xe_psum, e)
                    hold(e if isinstance(e, int) and e < 2 else 2 * e - 1)
                    pool.indirect_dma_start(XG[:, 0, :], None, xn_dram, bass.IndirectOffsetOnAxis(gidx[:, 0:1], 0)).then_inc(gathered, 16)
                    pool.indirect_dma_start(XG[0:CAP2, 1, :], None, xn_dram, bass.IndirectOffsetOnAxis(gidx[0:CAP2, 1:2], 0)).then_inc(gathered, 16)

                def scatter(e):
                    pool.wait_ge(y_ready, 2 * e + 2)
                    if not (isinstance(e, int) and e == 0):
                        pool.wait_ge(added, 32 * e)
                    hold(2 * e + 1 if isinstance(e, int) and e == NEXP - 1 else 2 * e + 2)
                    pool.indirect_dma_start(out, bass.IndirectOffsetOnAxis(sidx[:, 0:1], 0), Y[:, 0, :], None,
                                            compute_op=ALU.add).then_inc(added, 16)
                    pool.indirect_dma_start(out, bass.IndirectOffsetOnAxis(sidx[0:CAP2, 1:2], 0), Y[0:CAP2, 1, :], None,
                                            compute_op=ALU.add).then_inc(added, 16)

                pick(0)
                gather(0)
                pick(1)
                for half in range(2):
                    pool.wait_ge(so_added, 4 * half + 4)
                    pool.dma_start(out_tiles[:, 4 * half:4 * half + 4, :], X[:, 4 * half:4 * half + 4, :]).then_inc(so_out, 16)
                pool.wait_ge(so_out, 32)
                gather(1)
                if NEXP > 2:
                    pick(2)
                    scatter(0)
                    gather(2)
                    if NEXP > 3:
                        with pool.Fori(2, NEXP - 1) as e:
                            pick(e + 1)
                            scatter(e - 1)
                            gather(e + 1)
                else:
                    scatter(0)
                if NEXP > 2:
                    scatter(NEXP - 2)
                scatter(NEXP - 1)
                pool.wait_ge(added, 32 * NEXP)

            @block.tensor
            def _(pe):
                def make_list(e):
                    pe.wait_ge(oh_ready, TT * e + TT)
                    for t in range(TT):
                        pe.matmul(ps[:, 4, 320:326], OH[:, t, 0:P], RT[:, t, :], start=(t == 0), stop=(t == TT - 1))
                    for t in range(TT):
                        last = pe.matmul(ps[0:CAP2, 4, 328:334], OH[:, t, P:CAP], RT[:, t, :], start=(t == 0), stop=(t == TT - 1))
                    last.then_inc(ls_psum, 1)

                def turn_tokens(e):
                    pe.wait_ge(gathered, 32 * e + 32)
                    if not (isinstance(e, int) and e == 0):
                        pe.wait_ge(xel_done, 2 * e)
                    for k in range(G):
                        at = (k % 2) * CAP
                        pe.transpose(ps[:, 4 + k // 2, at:at + P], XG[:, 0, k * P:(k + 1) * P], ident[:, :])
                        last = pe.transpose(ps[:, 4 + k // 2, at + P:at + CAP], XG[0:CAP2, 1, k * P:(k + 1) * P],
                                            ident[0:CAP2, 0:CAP2])
                    last.then_inc(xe_psum, 1)

                def up(u, j, w, th, tl):
                    n = J * u + j
                    pe.wait_ge(hi_ready, n + 1)
                    pe.wait_ge(lo_ready, n + 1)
                    if not (isinstance(u, int) and n < 2):
                        pe.wait_ge(gf_done, n - 1)
                    for part in range(2):
                        dst = h_view(j, part, w)
                        for k in range(G):
                            begin = k == 0 and (part == 0 or w == HALF)
                            pe.matmul(dst, up_w(hi, j, part, k), th(k), start=begin, stop=False, skip_group_check=True)
                            pe.matmul(dst, up_w(hi, j, part, k), tl(k), start=False, stop=False, skip_group_check=True)
                            last = pe.matmul(dst, up_w(lo, j, part, k), th(k), start=False, stop=(k == G - 1), skip_group_check=True)
                    last.then_inc(h_psum, 1)

                def down(u, j, w):
                    pe.wait_ge(gl_done, J * u + j + 1)
                    for g in range(G):
                        if w == HALF:
                            dst, begin = ps[:, 4 + g, :], j == 0
                        else:
                            dst, begin = ps[:, g // 2, (g % 2) * CAP:(g % 2 + 1) * CAP], j == 0 and g % 2 == 0
                        end = j == J - 1
                        pe.matmul(dst, down_w(hi, j, g), Gh[:, j % 3, 0:w], start=begin, stop=False, skip_group_check=True)
                        pe.matmul(dst, down_w(hi, j, g), Gl[:, j % 3, 0:w], start=False, stop=False, skip_group_check=True)
                        last = pe.matmul(dst, down_w(lo, j, g), Gh[:, j % 3, 0:w], start=False, stop=end, skip_group_check=True)
                    last.then_inc(dn_done, 1)

                def turn_out(e):
                    pe.wait_ge(ot_copied, 2 * e + 2)
                    if not (isinstance(e, int) and e == 0):
                        pe.wait_ge(y_ready, 2 * e)
                    for g in range(G):
                        pe.transpose(ps[:, 6, g * P:(g + 1) * P], OT[:, g, 0:P], ident[:, :])
                        last = pe.transpose(ps[0:CAP2, 7, g * P:(g + 1) * P], OT[:, g, P:CAP], ident[:, :])
                    last.then_inc(y_psum, 1)

                def expert(e, last=False):
                    u = FIRST + e
                    pe.wait_ge(xel_done, 2 * e + 2)
                    for j in range(J):
                        up(u, j, CAP, lambda k: XEh[:, k, :], lambda k: XEl[:, k, :])
                        if j == 0 and not (isinstance(e, int) and e == 0):
                            turn_out(e - 1)
                        if j >= LAG:
                            down(u, j - LAG, CAP)
                        if j == 5 and not last:
                            make_list(e + 1)
                        if j == J - 2 and not last:
                            turn_tokens(e + 1)
                    for j in range(J - LAG, J):
                        down(u, j, CAP)

                make_list(0)
                pe.wait_ge(list_ready, 2)
                for half in range(2):
                    cols = slice(half * HALF, half * HALF + HALF)
                    if half:
                        pe.wait_ge(so_added, 4)
                    for j in range(J + LAG):
                        if j < J:
                            up(half, j, HALF, lambda k: XSh[:, k, cols], lambda k: XSl[:, k, cols])
                        if j >= LAG:
                            down(half, j - LAG, HALF)
                    pe.wait_ge(so_copied, 4 * half + 4)
                    for t in range(4):
                        for g in range(G):
                            last = pe.transpose(ps[:, t, g * P:(g + 1) * P], OT[:, g, t * P:(t + 1) * P], ident[:, :])
                        last.then_inc(so_turned, 1)
                pe.wait_ge(so_added, 8)
                turn_tokens(0)
                expert(0)
                expert(1, NEXP == 2)
                if NEXP > 2:
                    if NEXP > 3:
                        with pe.Fori(2, NEXP - 1) as e:
                            expert(e)
                    expert(NEXP - 1, True)
                turn_out(NEXP - 1)


_OUT = (T + CAP, D)


def kernel(**inputs):
    import numpy as np
    import concourse.bacc as bacc
    from concourse.bass_utils import run_bass_kernel_spmd as run

    a = {k: np.asarray(v) for k, v in inputs.items()}
    c = np.ascontiguousarray

    def feature_major(w):
        return c(w.T.reshape(G, P, w.shape[0]).transpose(1, 0, 2))

    def chunks(w1, w2):
        n = w1.shape[0]
        all_ = np.empty((n, J, P, CW), w1.dtype)
        up = w1.reshape(n, 2, J, P, G, P)
        for part in range(2):
            v = all_[:, :, :, part * G * P:(part + 1) * G * P].reshape(n, J, P, G, P)
            v[...] = up[:, 1 - part].transpose(0, 1, 4, 3, 2)
        all_[:, :, :, 2 * G * P:] = w2.reshape(n, D, J, P).transpose(0, 2, 3, 1)
        return all_

    ctx = a["ctx_1024"]
    named = {
        "x": c(a["x"]),
        "ctx_k": c(ctx.transpose(0, 2, 1).reshape(B, G, P, SK).transpose(0, 2, 1, 3)),
        "ctx_v": c(ctx),
        "wq": feature_major(a["L0_attn_wq_w"]), "wk": feature_major(a["L0_attn_wk_w"]),
        "wv": feature_major(a["L0_attn_wv_w"]), "wo": feature_major(a["L0_attn_wo_w"]),
        "bq": c(a["L0_attn_wq_b"].reshape(G, P).T), "bk": c(a["L0_attn_wk_b"].reshape(G, P).T),
        "bv": c(a["L0_attn_wv_b"].reshape(1, D)), "bo": c(a["L0_attn_wo_b"].reshape(1, D)),
        "wg": feature_major(a["L0_ffn_wg"]),
        "shared": chunks(a["L0_ffn_shared_w1"][None], a["L0_ffn_shared_w2"][None])[0],
        "experts": chunks(a["L0_ffn_expert_w1"], a["L0_ffn_expert_w2"]),
    }
    nc = bacc.Bacc("TRN2", target_bir_lowering=False, num_devices=1)
    args = [nc.dram_tensor(f"in_{k}", v.shape, mybir.dt.from_np(v.dtype), kind="ExternalInput").ap() for k, v in named.items()]
    out = nc.dram_tensor("out_rows", _OUT, F32, kind="ExternalOutput").ap()
    program(nc, *args, out)
    r = run(nc, [{f"in_{k}": v for k, v in named.items()}], core_ids=[0])
    return r.results[0]["out_rows"][0:T].reshape(B, SQ, D)
```

```python
from contextlib import ExitStack

import concourse.bass as bass
from concourse import mybir

F32 = mybir.dt.float32
BF16 = mybir.dt.bfloat16
I32 = mybir.dt.int32
ALU = mybir.AluOpType
ACT = mybir.ActivationFunctionType
AX = mybir.AxisListType

P = 128
B = 32
SQ = 32
SK = 257
D = 512
G = D // P
DH = 32
T = B * SQ
TT = T // P
NE = 64
TOPK = 8
FFN = 1536
J = FFN // P
CAP = 160
CAP2 = CAP - P
CW = 2 * G * P + D
PAIRS = J // 2
RING = J
LAG = 2
WIDTHS = (64, 96, 128, CAP)
HALF = T // 2
SCALE = float(DH) ** -0.5
EPS = 1e-5
FEPS = 1.1920928955078125e-07
MASKED = -(2.0 ** 126)


class Tally:

    def __init__(self, eng, sem):
        self.eng, self.sem, self.n = eng, sem, 0

    def did(self, ins):
        ins.then_inc(self.sem, 1)
        self.n += 1

    def settle(self):
        self.eng.wait_ge(self.sem, self.n)

    def then(self, ins):
        self.did(ins)
        self.settle()


def layernorm(dve, X, XN, stats, mv, small, done, std_ready, xn_ready):
    for t in range(TT):
        done.did(dve.bn_stats(stats[:, t, :], X[:, t, :]))
    done.settle()
    for t in range(TT):
        done.did(dve.bn_aggr(mv[:, t, :], stats[:, t, :]))
    done.settle()
    var, r, a = small[:, 0, :], small[:, 1, :], small[:, 2, :]
    done.then(dve.tensor_scalar(var, mv[:, :, 1], EPS, None, ALU.add))
    dve.wait_ge(std_ready, 1)
    done.then(dve.reciprocal(r, r))
    done.then(dve.tensor_tensor(a, r, r, ALU.mult))
    done.then(dve.tensor_tensor(a, a, var, ALU.mult))
    done.then(dve.tensor_scalar(a, a, -0.5, 1.5, ALU.mult, ALU.add))
    done.then(dve.tensor_tensor(r, r, a, ALU.mult))
    for t in range(TT):
        dve.tensor_scalar(XN[:, t, :], X[:, t, :], mv[:, t, 0:1], r[:, t:t + 1],
                          ALU.subtract, ALU.mult).then_inc(xn_ready, 1)


def transpose_tiles(pe, ps, XN, ident, xn_ready, xt_psum, xt_copied):
    for t in range(TT):
        pe.wait_ge(xn_ready, t + 1)
        if t >= 2:
            pe.wait_ge(xt_copied, t - 1)
        for g in range(G):
            last = pe.transpose(ps[:, t % 2, g * P:(g + 1) * P], XN[:, t, g * P:(g + 1) * P], ident[:, :])
        last.then_inc(xt_psum, 1)


def copy_tiles(act, ps, XT, small, ln_done, std_ready, xt_psum, xt_copied):
    act.wait_ge(ln_done, 2 * TT + 1)
    act.activation(small[:, 1, :], small[:, 0, :], ACT.Sqrt).then_inc(std_ready, 1)
    for t in range(TT):
        act.wait_ge(xt_psum, t + 1)
        act.activation(XT[:, :, t * P:(t + 1) * P], ps[:, t % 2, :].rearrange("p (g n) -> p g n", g=G),
                       ACT.Copy).then_inc(xt_copied, 1)


def program(nc, x, ctx_k, ctx_v, wq, wk, wv, wo, bq, bk, bv, bo, wg, shared, experts, out, NEXP=NE):
    root = ExitStack()
    with root:
        def allocator(stack):
            def sb(name, shape, dt=F32):
                return stack.enter_context(nc.sbuf_tensor(name, shape, dt))
            return sb

        def sem(name):
            return root.enter_context(nc.semaphore(name))

        sb = allocator(root)
        ps = root.enter_context(nc.psum_tensor("ps", [P, 8, 512], F32))
        xn_dram = nc.dram_tensor("xn_scratch", [T, D], F32, kind="Internal").ap()

        X = sb("X", [P, TT, D])
        ident = sb("ident", [P, P])
        stats = sb("stats", [P, TT, 6])
        mv = sb("mv", [P, TT, 2])
        small = sb("small", [P, 3, TT])
        x_dram = x.rearrange("b s d -> (b s) d").rearrange("(t p) d -> p t d", p=P)
        out_tiles = out[0:T, :].rearrange("(t p) d -> p t d", p=P)

        with ExitStack() as st:
            sb = allocator(st)
            XN = sb("a_XN", [P, TT, D])
            XT = sb("a_XT", [P, G, T])
            Q = sb("a_Q", [P, 4, G, P])
            K = sb("a_K", [P, 4, G, SK])
            V = sb("a_V", [P, 4, 3, D])
            PR = sb("a_PR", [P, 2, G, SK])
            PTa = sb("a_PTa", [P, 2, 2, G, P])
            PTb = sb("a_PTb", [1, 2, G, P])
            AT = sb("a_AT", [P, G, T])
            mx = sb("a_mx", [P, 2, G])
            nm = sb("a_nm", [P, 2, G])
            sm = sb("a_sm", [P, 2, G])
            rs = sb("a_rs", [P, 2, G])

            x_in = sem("a_x_in")
            k_in = [sem(f"a_k_in{i}") for i in range(4)]
            v_in = [sem(f"a_v_in{i}") for i in range(4)]
            ln_done = sem("a_ln_done")
            std_ready = sem("a_std_ready")
            xn_ready = sem("a_xn_ready")
            xt_psum = sem("a_xt_psum")
            xt_copied = sem("a_xt_copied")
            made = sem("a_made")
            zeroed = sem("a_zeroed")
            ident_ready = sem("a_ident_ready")
            q_ready = sem("a_q_ready")
            s_done = sem("a_s_done")
            max_done = sem("a_max_done")
            nm_done = sem("a_nm_done")
            exp_done = sem("a_exp_done")
            rec_done = sem("a_rec_done")
            pr_ready = sem("a_pr_ready")
            t_done = sem("a_t_done")
            pt_ready = sem("a_pt_ready")
            pv_done = sem("a_pv_done")
            at_ready = sem("a_at_ready")
            back_psum = sem("a_back_psum")
            x1_ready = sem("a_x1_ready")

            block = st.enter_context(nc.Block())

            @block.sync
            def _(sp):
                sp.dma_start(X[:, :, :], x_dram).then_inc(x_in, 16)

                def load(q, first):
                    for i in range(4):
                        b = 4 * q + i
                        if not first:
                            sp.wait_ge(s_done, b - 3)
                        sp.dma_start(K[:, i, :, :], ctx_k[b]).then_inc(k_in[i], 16)
                        if not first:
                            sp.wait_ge(pv_done, b - 3)
                        sp.dma_start(V[:, i, 0:2, :], ctx_v[b, 0:2 * P, :].rearrange("(k p) d -> p k d", p=P)).then_inc(v_in[i], 16)
                        sp.dma_start(V[0:1, i, 2, :], ctx_v[b, 2 * P:SK, :]).then_inc(v_in[i], 16)

                load(0, True)
                with sp.Fori(1, TT) as q:
                    load(q, False)

            @block.gpsimd
            def _(pool):
                pool.memset(ident[:, :], 0.0).then_inc(made, 1)
                pool.memset(Q[:, :, :, :], 0.0).then_inc(zeroed, 1)
                pool.wait_ge(made, 1)
                pool.affine_select(out=ident[:, :], in_=ident[:, :], compare_op=ALU.not_equal, fill=1.0, base=0,
                                   pattern=[[-1, P]], channel_multiplier=1).then_inc(ident_ready, 1)
                pool.wait_ge(zeroed, 1)

                def queries(q, first):
                    pool.wait_ge(xt_copied, q + 1)
                    for i in range(4):
                        b = 4 * q + i
                        if not first:
                            pool.wait_ge(s_done, b - 3)
                        for h in range(4):
                            r = slice(32 * h, 32 * h + 32)
                            pool.tensor_copy(Q[r, i, :, r], XT[r, :, bass.ds(P * q + SQ * i, SQ)]).then_inc(q_ready, 1)

                queries(0, True)
                with pool.Fori(1, TT) as q:
                    queries(q, False)

            @block.tensor
            def _(pe):
                pe.wait_ge(ident_ready, 1)
                transpose_tiles(pe, ps, XN, ident, xn_ready, xt_psum, xt_copied)
                pe.wait_ge(xt_copied, TT)

                def scores(b, i, q, first):
                    pe.wait_ge(q_ready, 4 * b + 4)
                    pe.wait_ge(k_in[i], 16 * q + 16)
                    if not (first and i == 0):
                        pe.wait_ge(exp_done, 4 * b)
                    for g in range(G):
                        last = pe.matmul(ps[:, g, 0:SK], Q[:, i, g, :], K[:, i, g, :], start=True, stop=True)
                    last.then_inc(s_done, 1)

                def turn(b, i):
                    pe.wait_ge(pr_ready, b + 1)
                    for g in range(G):
                        for k in range(2):
                            pe.transpose(ps[:, 4 + k, g * P:(g + 1) * P], PR[:, i % 2, g, k * P:(k + 1) * P], ident[:, :])
                        last = pe.transpose(ps[0:1, 6, g * P:(g + 1) * P], PR[:, i % 2, g, 2 * P:SK], ident[:, :])
                    last.then_inc(t_done, 1)

                def values(b, i, vcount):
                    pe.wait_ge(pt_ready, 2 * b + 2)
                    pe.wait_ge(v_in[i], vcount)
                    for g in range(G):
                        w = slice(g * P, (g + 1) * P)
                        for k in range(2):
                            pe.matmul(ps[:, 7, w], V[:, i, k, w], PTa[:, i % 2, k, g, :], start=(k == 0), stop=False)
                        last = pe.matmul(ps[:, 7, w], V[0:1, i, 2, w], PTb[0:1, i % 2, g, :], start=False, stop=True)
                    last.then_inc(pv_done, 1)

                def quad(q, first):
                    for i in range(4):
                        b = 4 * q + i
                        scores(b, i, q, first)
                        if not (first and i < 2):
                            if not (first and i < 3):
                                pe.wait_ge(at_ready, 4 * b - 8)
                            values(b - 2, (i - 2) % 4, 32 * q + 32 * (i >= 2))
                        if not (first and i < 1):
                            turn(b - 1, (i - 1) % 4)

                quad(0, True)
                with pe.Fori(1, TT) as q:
                    quad(q, False)
                pe.wait_ge(at_ready, 4 * (B - 2))
                values(B - 2, 2, 32 * TT)
                turn(B - 1, 3)
                pe.wait_ge(at_ready, 4 * (B - 1))
                values(B - 1, 3, 32 * TT)
                pe.wait_ge(at_ready, 4 * B)
                for t in range(TT):
                    if t >= 2:
                        pe.wait_ge(x1_ready, t - 1)
                    for g in range(G):
                        last = pe.transpose(ps[:, t % 2, g * P:(g + 1) * P], AT[:, g, t * P:(t + 1) * P], ident[:, :])
                    last.then_inc(back_psum, 1)

            @block.scalar
            def _(act):
                copy_tiles(act, ps, XT, small, ln_done, std_ready, xt_psum, xt_copied)

                def copy_pt(b, i):
                    act.wait_ge(t_done, b + 1)
                    act.activation(PTa[:, i % 2, :, :, :].rearrange("p k g n -> p (k g n)"),
                                   ps[:, 4:6, :].rearrange("p k n -> p (k n)"), ACT.Copy).then_inc(pt_ready, 1)
                    act.activation(PTb[0:1, i % 2, :, :].rearrange("p g n -> p (g n)"), ps[0:1, 6, :],
                                   ACT.Copy).then_inc(pt_ready, 1)

                def quad(q, first):
                    for i in range(4):
                        b = 4 * q + i
                        act.wait_ge(nm_done, b + 1)
                        if not (first and i < 2):
                            act.wait_ge(t_done, b - 1)
                        for g in range(G):
                            act.activation(PR[:, i % 2, g, :], ps[:, g, 0:SK], ACT.Exp, bias=nm[:, i % 2, g:g + 1],
                                           scale=SCALE, accum_out=sm[:, i % 2, g:g + 1]).then_inc(exp_done, 1)
                        if not (first and i < 1):
                            if not (first and i < 3):
                                act.wait_ge(pv_done, b - 2)
                            copy_pt(b - 1, (i - 1) % 4)

                quad(0, True)
                with act.Fori(1, TT) as q:
                    quad(q, False)
                act.wait_ge(pv_done, B - 2)
                copy_pt(B - 1, 3)

            @block.vector
            def _(dve):
                dve.wait_ge(x_in, 16)
                layernorm(dve, X, XN, stats, mv, small, Tally(dve, ln_done), std_ready, xn_ready)

                def diagonal(b, q, i):
                    dve.wait_ge(pv_done, b + 1)
                    for h in range(4):
                        r = slice(32 * h, 32 * h + 32)
                        dve.tensor_copy(AT[r, :, bass.ds(P * q + SQ * i, SQ)],
                                        ps[r, 7, :].rearrange("p (g n) -> p g n", g=G)[:, :, r]).then_inc(at_ready, 1)

                def quad(q, first):
                    for i in range(4):
                        b = 4 * q + i
                        k = i % 2
                        dve.wait_ge(s_done, b + 1)
                        dve.tensor_reduce(mx[:, k, :], ps[:, 0:G, 0:SK], AX.X, ALU.max).then_inc(max_done, 1)
                        dve.wait_ge(max_done, b + 1)
                        if not (first and i < 2):
                            dve.wait_ge(exp_done, 4 * b - 4)
                        dve.tensor_scalar(nm[:, k, :], mx[:, k, :], -SCALE, None, ALU.mult).then_inc(nm_done, 1)
                        if not (first and i < 2):
                            if i < 2:
                                diagonal(b - 2, q - 1, i + 2)
                            else:
                                diagonal(b - 2, q, i - 2)
                        dve.wait_ge(exp_done, 4 * b + 4)
                        dve.reciprocal(rs[:, k, :], sm[:, k, :]).then_inc(rec_done, 1)
                        dve.wait_ge(rec_done, b + 1)
                        dve.tensor_tensor(PR[:, k, :, :], PR[:, k, :, :], rs[:, k, :].rearrange("p (g o) -> p g o", o=1).to_broadcast([P, G, SK]),
                                          ALU.mult).then_inc(pr_ready, 1)

                quad(0, True)
                with dve.Fori(1, TT) as q:
                    quad(q, False)
                diagonal(B - 2, TT - 1, 2)
                diagonal(B - 1, TT - 1, 3)
                for t in range(TT):
                    dve.wait_ge(back_psum, t + 1)
                    dve.tensor_tensor(X[:, t, :], X[:, t, :], ps[:, t % 2, :], ALU.add).then_inc(x1_ready, 1)
                dve.wait_ge(x1_ready, TT)

        with ExitStack() as st:
            sb = allocator(st)
            XN = sb("b_XN", [P, TT, D])
            XT = sb("b_XT", [P, G, T])
            W = sb("b_W", [P, 4, G, D])
            bqk = sb("b_bqk", [P, 2, G])
            bvo = sb("b_bvo", [P, 2, D])
            QT = sb("b_QT", [P, G, T])
            KT = sb("b_KT", [P, G, T])
            VV = sb("b_VV", [P, TT, D])
            Q = sb("b_Q", [P, 2, 4, G, P])
            mask = sb("b_mask", [1, 1, T], BF16)
            ones = sb("b_ones", [1, P], BF16)
            S = sb("b_S", [P, 2, 4 * G, SQ])
            PT = sb("b_PT", [P, 2, G, P])
            AT = sb("b_AT", [P, G, T])
            mx = sb("b_mx", [P, 4 * G])
            sm = sb("b_sm", [P, 4 * G])

            w_in = sem("b_w_in")
            ln_done = sem("b_ln_done")
            std_ready = sem("b_std_ready")
            xn_ready = sem("b_xn_ready")
            xt_psum = sem("b_xt_psum")
            xt_copied = sem("b_xt_copied")
            consts = sem("b_consts")
            mask_ready = sem("b_mask_ready")
            proj_psum = sem("b_proj_psum")
            proj_even = sem("b_proj_even")
            proj_odd = sem("b_proj_odd")
            q_ready = sem("b_q_ready")
            s_done = sem("b_s_done")
            soft = sem("b_soft")
            sub_done = sem("b_sub_done")
            exp_done = sem("b_exp_done")
            pr_ready = sem("b_pr_ready")
            t_done = sem("b_t_done")
            pt_ready = sem("b_pt_ready")
            pv_done = sem("b_pv_done")
            at_ready = sem("b_at_ready")
            o_psum = sem("b_o_psum")
            o_added = sem("b_o_added")
            x2_done = sem("b_x2_done")

            block = st.enter_context(nc.Block())

            @block.sync
            def _(sp):
                for i, w in enumerate((wq, wk, wv, wo)):
                    sp.dma_start(W[:, i, :, :], w).then_inc(w_in, 16)
                for i, v in enumerate((bq, bk)):
                    sp.dma_start(bqk[:, i, :], v).then_inc(w_in, 16)
                for i, v in enumerate((bv, bo)):
                    sp.dma_start(bvo[:, i, :], v.to_broadcast([P, D])).then_inc(w_in, 16)

            @block.gpsimd
            def _(pool):
                pool.memset(Q[:, :, :, :, :], 0.0).then_inc(consts, 1)
                pool.memset(ones[:, :], 1.0).then_inc(consts, 1)
                pool.wait_ge(consts, 2)
                for t in range(TT):
                    pool.wait_ge(proj_even, 4 * (t // 4) + 4)
                    if t >= 2:
                        pool.wait_ge(s_done, t - 1)
                    for h in range(4):
                        r = slice(32 * h, 32 * h + 32)
                        pool.tensor_copy(Q[r, t % 2, :, :, r].rearrange("p b g n -> p g b n"),
                                         QT[r, :, t * P:(t + 1) * P].rearrange("p g (b n) -> p g b n", b=4)).then_inc(q_ready, 1)

            @block.tensor
            def _(pe):
                transpose_tiles(pe, ps, XN, ident, xn_ready, xt_psum, xt_copied)
                pe.wait_ge(xt_copied, TT)
                pe.wait_ge(w_in, 16 * 8)
                n = 0

                def bank():
                    if n >= 4:
                        pe.wait_ge(proj_even if n % 2 == 0 else proj_odd, (n - 4) // 2 + 1)
                    return ps[:, 2 + n % 4, :]

                for half in range(2):
                    cols = slice(half * HALF, half * HALF + HALF)
                    for o in range(G):
                        for i in range(2):
                            dst = bank()
                            for k in range(G):
                                last = pe.matmul(dst, W[:, i, k, o * P:(o + 1) * P], XT[:, k, cols], start=(k == 0), stop=(k == G - 1))
                            last.then_inc(proj_psum, 1)
                            n += 1
                for t in range(TT):
                    dst = bank()
                    for k in range(G):
                        last = pe.matmul(dst, XT[:, k, t * P:(t + 1) * P], W[:, 2, k, :], start=(k == 0), stop=(k == G - 1))
                    last.then_inc(proj_psum, 1)
                    n += 1
                pe.wait_ge(proj_odd, 12)
                pe.wait_ge(proj_even, 12)
                pe.wait_ge(mask_ready, 1)

                def scores(t):
                    pe.wait_ge(q_ready, 4 * t + 4)
                    if t >= 2:
                        pe.wait_ge(sub_done, t - 1)
                    bk_ = ps[:, t % 2, :]
                    pe.matmul(bk_, ones[:, :], mask[0:1, :, t * P:(t + 1) * P].to_broadcast([1, G, P]),
                              start=True, stop=False, skip_group_check=True)
                    for g in range(G):
                        for b in range(4):
                            c = g * P + b * SQ
                            last = pe.matmul(bk_[:, c:c + SQ], Q[:, t % 2, b, g, :], KT[:, g, t * P + b * SQ:t * P + (b + 1) * SQ],
                                             start=False, stop=(g == 3 and b == 3), skip_group_check=True)
                    last.then_inc(s_done, 1)

                def turn(t):
                    pe.wait_ge(pr_ready, t + 1)
                    if t >= 1:
                        pe.wait_ge(pt_ready, t)
                    for g in range(G):
                        last = pe.transpose(ps[:, 2, g * P:(g + 1) * P], S[:, t % 2, 4 * g:4 * g + 4, :].rearrange("p b n -> p (b n)"), ident[:, :])
                    last.then_inc(t_done, 1)

                def values(t):
                    pe.wait_ge(pt_ready, t + 1)
                    if t >= 1:
                        pe.wait_ge(at_ready, 4 * t)
                    for b in range(4):
                        r = slice(32 * b, 32 * b + 32)
                        for g in range(G):
                            last = pe.matmul(ps[:, 4 + b, g * P:(g + 1) * P], VV[r, t, g * P:(g + 1) * P], PT[r, t % 2, g, :],
                                             start=True, stop=True)
                    last.then_inc(pv_done, 1)

                for t in range(TT + 2):
                    if t < TT:
                        scores(t)
                    if t >= 2:
                        values(t - 2)
                    if 1 <= t <= TT:
                        turn(t - 1)
                pe.wait_ge(at_ready, 4 * TT)
                for t in range(TT):
                    if t >= 2:
                        pe.wait_ge(o_added, t - 1)
                    for k in range(G):
                        last = pe.matmul(ps[:, t % 2, :], AT[:, k, t * P:(t + 1) * P], W[:, 3, k, :], start=(k == 0), stop=(k == G - 1))
                    last.then_inc(o_psum, 1)

            @block.scalar
            def _(act):
                copy_tiles(act, ps, XT, small, ln_done, std_ready, xt_psum, xt_copied)
                act.wait_ge(w_in, 16 * 8)
                n = 0
                for half in range(2):
                    for o in range(G):
                        act.wait_ge(proj_psum, n + 1)
                        act.activation(QT[:, o, half * HALF:half * HALF + HALF], ps[:, 2 + n % 4, :], ACT.Identity,
                                       bias=bqk[:, 0, o:o + 1]).then_inc(proj_even, 1)
                        n += 2
                for t in range(0, TT, 2):
                    act.wait_ge(proj_psum, n + 1)
                    act.activation(VV[:, t, :], ps[:, 2 + n % 4, :], ACT.Copy).then_inc(proj_even, 1)
                    n += 2
                for t in range(TT + 1):
                    if t < TT:
                        act.wait_ge(sub_done, t + 1)
                        act.activation(S[:, t % 2, :, :], S[:, t % 2, :, :], ACT.Exp, scale=SCALE).then_inc(exp_done, 1)
                    if t >= 1:
                        act.wait_ge(t_done, t)
                        if t >= 3:
                            act.wait_ge(pv_done, t - 2)
                        act.activation(PT[:, (t - 1) % 2, :, :].rearrange("p g n -> p (g n)"), ps[:, 2, :], ACT.Copy).then_inc(pt_ready, 1)

            @block.vector
            def _(dve):
                layernorm(dve, X, XN, stats, mv, small, Tally(dve, ln_done), std_ready, xn_ready)
                dve.wait_ge(xt_copied, TT)
                dve.tensor_scalar(mask[0:1, 0, :], XT[0:1, 0, :], 0.0, MASKED, ALU.is_equal, ALU.mult).then_inc(mask_ready, 1)
                dve.wait_ge(w_in, 16 * 8)
                n = 1
                for half in range(2):
                    for o in range(G):
                        dve.wait_ge(proj_psum, n + 1)
                        dve.tensor_scalar(KT[:, o, half * HALF:half * HALF + HALF], ps[:, 2 + n % 4, :], bqk[:, 1, o:o + 1], None,
                                          ALU.add).then_inc(proj_odd, 1)
                        n += 2
                for t in range(1, TT, 2):
                    dve.wait_ge(proj_psum, n + 1)
                    dve.tensor_tensor(VV[:, t, :], ps[:, 2 + n % 4, :], bvo[:, 0, :], ALU.add).then_inc(proj_odd, 1)
                    n += 2
                chain = Tally(dve, soft)
                dve.wait_ge(proj_even, 12)
                for t in range(0, TT, 2):
                    chain.did(dve.tensor_tensor(VV[:, t, :], VV[:, t, :], bvo[:, 0, :], ALU.add))
                for t in range(TT):
                    chain.did(dve.tensor_tensor(X[:, t, :], X[:, t, :], bvo[:, 1, :], ALU.add))
                chain.settle()

                def diagonal(t):
                    dve.wait_ge(pv_done, t + 1)
                    for h in range(4):
                        r = slice(32 * h, 32 * h + 32)
                        dve.tensor_copy(AT[r, :, t * P:(t + 1) * P].rearrange("p g (b n) -> p g b n", b=4),
                                        ps[r, 4:8, :].rearrange("p b (g n) -> p g b n", g=G)[:, :, :, r]).then_inc(at_ready, 1)

                for t in range(TT):
                    dve.wait_ge(s_done, t + 1)
                    bk_ = ps[:, t % 2, :].rearrange("p (c n) -> p c n", n=SQ)
                    bc = lambda v: v[:, :].rearrange("p (c o) -> p c o", o=1).to_broadcast([P, 4 * G, SQ])
                    chain.then(dve.tensor_reduce(mx[:, :], bk_, AX.X, ALU.max))
                    if t >= 2:
                        dve.wait_ge(t_done, t - 1)
                    dve.tensor_tensor(S[:, t % 2, :, :], bk_, bc(mx), ALU.subtract).then_inc(sub_done, 1)
                    if t >= 2:
                        diagonal(t - 2)
                    dve.wait_ge(exp_done, t + 1)
                    chain.then(dve.tensor_reduce(sm[:, :], S[:, t % 2, :, :], AX.X, ALU.add))
                    chain.then(dve.reciprocal(sm[:, :], sm[:, :]))
                    dve.tensor_tensor(S[:, t % 2, :, :], S[:, t % 2, :, :], bc(sm), ALU.mult).then_inc(pr_ready, 1)
                    dve.wait_ge(pr_ready, t + 1)
                diagonal(TT - 2)
                diagonal(TT - 1)
                for t in range(TT):
                    dve.wait_ge(o_psum, t + 1)
                    dve.tensor_tensor(X[:, t, :], X[:, t, :], ps[:, t % 2, :], ALU.add).then_inc(o_added, 1)
                dve.wait_ge(o_added, TT)

        sb = allocator(root)
        RK = sb("RK", [P, NE, TT])
        WS = sb("WS", [P, NE, TT, 3], BF16)
        XT = sb("XT", [P, G, T])
        width = sb("width", [1, NE], I32)
        ring = sb("ring", [P, PAIRS, 2, CW])
        ring_in = [sem(f"ring_in{i}") for i in range(PAIRS)]
        with ExitStack() as st:
            sb = allocator(st)
            XN = sb("c_XN", [P, TT, D])
            wgs = sb("c_wg", [P, G, NE])
            L = sb("c_L", [P, TT, NE])
            M = sb("c_M", [P, TT, NE])
            sel = sb("c_sel", [P, TT, NE])
            selb = sb("c_selb", [P, TT, NE], BF16)
            before = sb("c_before", [P, P], BF16)
            ones = sb("c_ones", [P, P], BF16)
            top = sb("c_top", [P, TT, 8])
            red = sb("c_red", [P, 3, TT])
            over = sb("c_over", [1, 3, NE])
            zero = sb("c_zero", [P, D])

            wg_in = sem("c_wg_in")
            ln_done = sem("c_ln_done")
            std_ready = sem("c_std_ready")
            xn_ready = sem("c_xn_ready")
            xt_psum = sem("c_xt_psum")
            xt_copied = sem("c_xt_copied")
            consts = sem("c_consts")
            consts2 = sem("c_consts2")
            lg_psum = sem("c_lg_psum")
            shifted = sem("c_shifted")
            exped = sem("c_exped")
            chain_s = sem("c_chain")
            sel_ready = sem("c_sel_ready")
            rk_psum = sem("c_rk_psum")
            scratch_out = sem("c_scratch_out")

            block = st.enter_context(nc.Block())

            @block.sync
            def _(sp):
                sp.dma_start(wgs[:, :, :], wg).then_inc(wg_in, 16)
                for i in range(PAIRS):
                    sp.dma_start(ring[:, i, :, :], shared[i]).then_inc(ring_in[i], 16)
                sp.wait_ge(xn_ready, TT)
                sp.dma_start(xn_dram.rearrange("(t p) d -> p t d", p=P), XN[:, :, :]).then_inc(scratch_out, 16)
                sp.wait_ge(consts, 3)
                sp.dma_start(out[T:T + P, :], zero[:, :]).then_inc(scratch_out, 16)
                sp.dma_start(out[T + P:T + CAP, :], zero[0:CAP2, :]).then_inc(scratch_out, 16)
                sp.wait_ge(scratch_out, 48)

            @block.gpsimd
            def _(pool):
                pool.memset(before[:, :], 1.0).then_inc(consts, 1)
                pool.memset(ones[:, :], 1.0).then_inc(consts, 1)
                pool.memset(zero[:, :], 0.0).then_inc(consts, 1)
                pool.wait_ge(consts, 3)
                pool.affine_select(out=before[:, :], in_=before[:, :], compare_op=ALU.is_gt, fill=0.0, base=0,
                                   pattern=[[1, P]], channel_multiplier=-1).then_inc(consts2, 1)

            @block.tensor
            def _(pe):
                transpose_tiles(pe, ps, XN, ident, xn_ready, xt_psum, xt_copied)
                pe.wait_ge(xt_copied, TT)
                pe.wait_ge(wg_in, 16)
                for t in range(TT):
                    for k in range(G):
                        last = pe.matmul(ps[:, 2, t * NE:(t + 1) * NE], XT[:, k, t * P:(t + 1) * P], wgs[:, k, :],
                                         start=(k == 0), stop=(k == G - 1))
                last.then_inc(lg_psum, 1)
                pe.wait_ge(consts2, 1)
                pe.wait_ge(sel_ready, 1)
                for t in range(TT):
                    for s in range(t + 1):
                        last = pe.matmul(ps[:, 3, t * NE:(t + 1) * NE], before[:, :] if s == t else ones[:, :], selb[:, s, :],
                                         start=(s == 0), stop=(s == t))
                for t in range(TT):
                    last = pe.matmul(ps[:, 4, 0:NE], ones[:, :], selb[:, t, :], start=(t == 0), stop=(t == TT - 1))
                last.then_inc(rk_psum, 1)

            @block.scalar
            def _(act):
                copy_tiles(act, ps, XT, small, ln_done, std_ready, xt_psum, xt_copied)
                act.wait_ge(xt_copied, TT)
                act.wait_ge(shifted, 1)
                act.activation(L[:, :, :], L[:, :, :], ACT.Exp).then_inc(exped, 1)

            @block.vector
            def _(dve):
                layernorm(dve, X, XN, stats, mv, small, Tally(dve, ln_done), std_ready, xn_ready)
                chain = Tally(dve, chain_s)
                bc = lambda v: v.rearrange("p (t o) -> p t o", o=1).to_broadcast([P, TT, NE])
                dve.wait_ge(lg_psum, 1)
                lg = ps[:, 2, :].rearrange("p (t e) -> p t e", e=NE)
                chain.then(dve.tensor_reduce(red[:, 0, :], lg, AX.X, ALU.max))
                dve.tensor_tensor(L[:, :, :], lg, bc(red[:, 0, :]), ALU.subtract).then_inc(shifted, 1)
                dve.wait_ge(exped, 1)
                chain.then(dve.tensor_reduce(red[:, 1, :], L[:, :, :], AX.X, ALU.add))
                chain.then(dve.reciprocal(red[:, 1, :], red[:, 1, :]))
                chain.then(dve.tensor_tensor(L[:, :, :], L[:, :, :], bc(red[:, 1, :]), ALU.mult))
                for t in range(TT):
                    chain.did(dve.max(top[:, t, :], L[:, t, :]))
                chain.settle()
                for t in range(TT):
                    chain.did(dve.match_replace(M[:, t, :], top[:, t, :], L[:, t, :], -1.0))
                chain.settle()
                chain.then(dve.tensor_scalar(sel[:, :, :], M[:, :, :], 0.0, None, ALU.is_lt))
                dve.tensor_copy(selb[:, :, :], sel[:, :, :]).then_inc(sel_ready, 1)
                chain.did(dve.tensor_reduce(red[:, 2, :], top[:, :, :], AX.X, ALU.add))
                chain.then(dve.tensor_tensor(L[:, :, :], L[:, :, :], sel[:, :, :], ALU.mult))
                chain.then(dve.tensor_scalar(red[:, 2, :], red[:, 2, :], FEPS, None, ALU.max))
                chain.then(dve.reciprocal(red[:, 2, :], red[:, 2, :]))
                chain.then(dve.tensor_tensor(L[:, :, :], L[:, :, :], bc(red[:, 2, :]), ALU.mult))
                for i in range(3):
                    part = WS[:, 0:NE, :, i].rearrange("p e t -> p t e")
                    chain.then(dve.tensor_copy(part, L[:, :, :]))
                    if i < 2:
                        chain.then(dve.tensor_tensor(L[:, :, :], L[:, :, :], part, ALU.subtract))
                dve.wait_ge(rk_psum, 1)
                rk = RK[:, 0:NE, :].rearrange("p e t -> p t e")
                chain.then(dve.scalar_tensor_tensor(rk, ps[:, 3, :].rearrange("p (t e) -> p t e", e=NE), 1.0, sel[:, :, :],
                                                    ALU.add, ALU.mult))
                chain.then(dve.tensor_scalar(RK[:, 0:NE, :], RK[:, 0:NE, :], -1.0, None, ALU.add))
                for i in range(3):
                    chain.did(dve.tensor_scalar(over[:, i, :], ps[0:1, 4, 0:NE], float(WIDTHS[i]), None, ALU.is_gt))
                chain.settle()
                chain.then(dve.tensor_tensor(over[:, 0, :], over[:, 0, :], over[:, 1, :], ALU.add))
                chain.then(dve.tensor_tensor(width[:, :], over[:, 0, :], over[:, 2, :], ALU.add))

        with ExitStack() as st:
            sb = allocator(st)
            SL = sb("d_SL", [P, 2, HALF])
            GU = sb("d_GU", [P, 3, HALF])
            OT = sb("d_OT", [P, G, CAP])
            iota = sb("d_iota", [P, CAP], BF16)
            tick = sb("d_tick", [P, 1])
            RKe = sb("d_RKe", [P, TT])
            OH = sb("d_OH", [P, TT, CAP], BF16)
            RT = sb("d_RT", [P, TT, 6], BF16)
            LS = sb("d_LS", [P, 2, 6])
            slot = sb("d_slot", [P, 2])
            tk = sb("d_tk", [P, 4, 2])
            gidx = sb("d_gidx", [P, 2], I32)
            sidxn = sb("d_sidxn", [P, 2], I32)
            sidx = sb("d_sidx", [P, 2], I32)
            gaten = sb("d_gaten", [P, 2])
            gate = sb("d_gate", [P, 2])
            XG = sb("d_XG", [P, 2, D])
            XE = sb("d_XE", [P, G, CAP])
            Y = sb("d_Y", [P, 2, D])

            h_psum = sem("d_h_psum")
            silu_done = sem("d_silu_done")
            gu_done = sem("d_gu_done")
            dn_done = sem("d_dn_done")
            so_added = sem("d_so_added")
            so_out = sem("d_so_out")
            ls_clear = sem("d_ls_clear")
            consts = sem("d_consts")
            picked = sem("d_picked")
            ticked = sem("d_ticked")
            oh_ready = sem("d_oh_ready")
            ls_psum = sem("d_ls_psum")
            list_s = sem("d_list")
            list_ready = sem("d_list_ready")
            list_kept = sem("d_list_kept")
            gathered = sem("d_gathered")
            xe_psum = sem("d_xe_psum")
            xe_done = sem("d_xe_done")
            ot_copied = sem("d_ot_copied")
            y_psum = sem("d_y_psum")
            y_ready = sem("d_y_ready")
            added = sem("d_added")

            block = st.enter_context(nc.Block())

            FIRST = 2

            def up_w(j, part, k):
                at = (part * G + k) * P
                return ring[:, j // 2, j % 2, at:at + P]

            def down_w(j):
                return ring[:, j // 2, j % 2, 2 * G * P:CW]

            def h_view(j, part, w):
                if w == HALF:
                    return ps[:, 2 * (j % 2) + part, :]
                return ps[:, 2 + j % 2, part * CAP:part * CAP + w]

            def pair(bank):
                return ps[:, bank, 0:2 * CAP].rearrange("p (k n) -> p k n", k=2)

            def is_static(e, n):
                return isinstance(e, int) and e == n

            @block.sync
            def _(sp):
                def load(src, u, i):
                    sp.wait_ge(dn_done, J * (u - 1) + 2 * i + 2)
                    sp.dma_start(ring[:, i, :, :], src).then_inc(ring_in[i], 16)

                for i in range(PAIRS):
                    load(shared[i], 1, i)
                with sp.Fori(0, NEXP) as e:
                    for i in range(PAIRS):
                        load(experts[e, i], FIRST + e, i)

            @block.scalar
            def _(act):
                def silu(u, j, w):
                    n = J * u + j
                    act.wait_ge(h_psum, n + 1)
                    if not (isinstance(u, int) and n < 2):
                        act.wait_ge(gu_done, n - 1)
                    act.activation(SL[:, j % 2, 0:w], h_view(j, 0, w), ACT.Silu).then_inc(silu_done, 1)

                def tokens(e):
                    act.wait_ge(xe_psum, e + 1)
                    if not is_static(e, 0):
                        act.wait_ge(h_psum, J * (FIRST + e))
                    for i in range(2):
                        act.activation(XE[:, 2 * i:2 * i + 2, :], pair(4 + i), ACT.Copy).then_inc(xe_done, 1)

                def take_out(e):
                    act.wait_ge(dn_done, J * (FIRST + e) + J)
                    for i in range(2):
                        act.activation(OT[:, 2 * i:2 * i + 2, :], pair(i), ACT.Copy).then_inc(ot_copied, 1)

                def weigh(e):
                    act.wait_ge(y_psum, e + 1)
                    act.wait_ge(list_kept, 2 * e + 2)
                    if not is_static(e, 0):
                        act.wait_ge(added, 32 * e)
                    act.activation(Y[:, 0, :], ps[:, 6, :], ACT.Copy, scale=gate[:, 0:1]).then_inc(y_ready, 1)
                    act.activation(Y[0:CAP2, 1, :], ps[0:CAP2, 7, :], ACT.Copy, scale=gate[0:CAP2, 1:2]).then_inc(y_ready, 1)

                def expert(e, last=False):
                    if not is_static(e, 0):
                        take_out(e - 1)
                    for j in range(J):
                        silu(FIRST + e, j, CAP)
                        if j == 1 and not is_static(e, 0):
                            weigh(e - 1)
                    if not last:
                        tokens(e + 1)

                for half in range(2):
                    for j in range(J):
                        silu(half, j, HALF)
                tokens(0)
                expert(0)
                expert(1, NEXP == 2)
                if NEXP > 2:
                    if NEXP > 3:
                        with act.Fori(2, NEXP - 1) as e:
                            expert(e)
                    expert(NEXP - 1, True)
                take_out(NEXP - 1)
                weigh(NEXP - 1)

            @block.vector
            def _(dve):
                def product(u, j, w):
                    n = J * u + j
                    dve.wait_ge(silu_done, n + 1)
                    if not (isinstance(u, int) and n < 3):
                        dve.wait_ge(dn_done, n - 2)
                    dve.tensor_tensor(GU[:, j % 3, 0:w], SL[:, j % 2, 0:w], h_view(j, 1, w), ALU.mult).then_inc(gu_done, 1)

                def onehot(e, tiles):
                    dve.wait_ge(picked, 2 * e + 2)
                    for t in tiles:
                        dve.tensor_scalar(OH[:, t, :], iota[:, :], RKe[:, t:t + 1], None, ALU.is_equal).then_inc(oh_ready, 1)

                lists = Tally(dve, list_s)
                LIST_STEPS = 7

                def read_list(e):
                    lists.n = LIST_STEPS * e
                    dve.wait_ge(ls_psum, e + 1)
                    lists.did(dve.tensor_copy(LS[:, 0, :], ps[:, 4, 320:326]))
                    lists.did(dve.tensor_copy(LS[0:CAP2, 1, :], ps[0:CAP2, 4, 328:334]))
                    lists.settle()
                    token, a = tk[:, 0, :], tk[:, 1, :]
                    lists.did(dve.tensor_reduce(token, LS[:, :, 0:2], AX.X, ALU.add))
                    lists.did(dve.tensor_reduce(gaten[:, :], LS[:, :, 3:6], AX.X, ALU.add))
                    lists.then(dve.tensor_tensor(a, LS[:, :, 2], slot[:, :], ALU.mult))
                    lists.then(dve.tensor_tensor(a, a, token, ALU.subtract))
                    lists.then(dve.tensor_tensor(a, slot[:, :], a, ALU.subtract))
                    if not is_static(e, 0):
                        dve.wait_ge(gathered, 32 * e)
                    dve.tensor_copy(sidxn[:, :], a).then_inc(list_ready, 1)
                    dve.tensor_copy(gidx[:, :], token).then_inc(list_ready, 1)
                    dve.wait_ge(list_ready, 2 * e + 2)

                def keep_list(e):
                    if not is_static(e, 0):
                        dve.wait_ge(added, 32 * e)
                        dve.wait_ge(y_ready, 2 * e)
                    dve.tensor_copy(sidx[:, :], sidxn[:, :]).then_inc(list_kept, 1)
                    dve.tensor_copy(gate[:, :], gaten[:, :]).then_inc(list_kept, 1)
                    dve.wait_ge(list_kept, 2 * e + 2)

                def expert(e, last=False):
                    for j in range(J):
                        product(FIRST + e, j, CAP)
                        if j < 4 and not last:
                            onehot(e + 1, (2 * j, 2 * j + 1))
                        if j == 6:
                            if not is_static(e, 0):
                                keep_list(e)
                            if not last:
                                read_list(e + 1)

                dve.memset(LS[:, :, :], 0.0).then_inc(ls_clear, 1)
                dve.wait_ge(ls_clear, 1)
                dve.wait_ge(consts, 5)
                onehot(0, range(TT))
                read_list(0)
                keep_list(0)
                for half in range(2):
                    for j in range(J):
                        product(half, j, HALF)
                    dve.wait_ge(dn_done, J * half + J)
                    for t in range(4):
                        row = 4 * half + t
                        dve.tensor_tensor(X[:, row, :], X[:, row, :], ps[:, 4 + t, :], ALU.add).then_inc(so_added, 1)
                expert(0)
                expert(1, NEXP == 2)
                if NEXP > 2:
                    if NEXP > 3:
                        with dve.Fori(2, NEXP - 1) as e:
                            expert(e)
                    expert(NEXP - 1, True)

            @block.gpsimd
            def _(pool):
                exact = dict(allow_small_or_imprecise_dtypes=True)
                pool.iota(iota[:, :], [[1, CAP]], base=0, channel_multiplier=0, **exact).then_inc(consts, 1)
                pool.iota(slot[:, :], [[P, 2]], base=T, channel_multiplier=1, **exact).then_inc(consts, 1)
                pool.iota(RT[:, :, 0], [[P, TT]], base=0, channel_multiplier=0, **exact).then_inc(consts, 1)
                pool.iota(RT[:, :, 1], [[0, TT]], base=0, channel_multiplier=1, **exact).then_inc(consts, 1)
                pool.memset(RT[:, :, 2], 1.0).then_inc(consts, 1)
                pool.wait_ge(consts, 5)

                def pick(e):
                    if not (isinstance(e, int) and e == 0):
                        pool.wait_ge(ls_psum, e)
                    pool.tensor_copy(RKe[:, :], RK[:, bass.ds(e, 1), :].rearrange("p o t -> p (o t)")).then_inc(picked, 1)
                    pool.tensor_copy(RT[:, :, 3:6], WS[:, bass.ds(e, 1), :, :].rearrange("p o t c -> p (o t) c")).then_inc(picked, 1)

                def hold(before):
                    if not (isinstance(before, int) and before == 0):
                        pool.wait_ge(ticked, before)
                    pool.tensor_tensor(tick[:, :], iota[:, 0:1], iota[:, 0:1], ALU.add).then_inc(ticked, 1)

                def gather(e):
                    pool.wait_ge(list_ready, 2 * e + 2)
                    if not (isinstance(e, int) and e == 0):
                        pool.wait_ge(xe_psum, e)
                    hold(e if isinstance(e, int) and e < 2 else 2 * e - 1)
                    pool.indirect_dma_start(XG[:, 0, :], None, xn_dram, bass.IndirectOffsetOnAxis(gidx[:, 0:1], 0)).then_inc(gathered, 16)
                    pool.indirect_dma_start(XG[0:CAP2, 1, :], None, xn_dram, bass.IndirectOffsetOnAxis(gidx[0:CAP2, 1:2], 0)).then_inc(gathered, 16)

                def scatter(e):
                    pool.wait_ge(y_ready, 2 * e + 2)
                    if not (isinstance(e, int) and e == 0):
                        pool.wait_ge(added, 32 * e)
                    hold(2 * e + 1 if isinstance(e, int) and e == NEXP - 1 else 2 * e + 2)
                    pool.indirect_dma_start(out, bass.IndirectOffsetOnAxis(sidx[:, 0:1], 0), Y[:, 0, :], None,
                                            compute_op=ALU.add).then_inc(added, 16)
                    pool.indirect_dma_start(out, bass.IndirectOffsetOnAxis(sidx[0:CAP2, 1:2], 0), Y[0:CAP2, 1, :], None,
                                            compute_op=ALU.add).then_inc(added, 16)

                pick(0)
                gather(0)
                pick(1)
                for half in range(2):
                    pool.wait_ge(so_added, 4 * half + 4)
                    pool.dma_start(out_tiles[:, 4 * half:4 * half + 4, :], X[:, 4 * half:4 * half + 4, :]).then_inc(so_out, 16)
                pool.wait_ge(so_out, 32)
                gather(1)
                if NEXP > 2:
                    pick(2)
                    scatter(0)
                    gather(2)
                    if NEXP > 3:
                        with pool.Fori(2, NEXP - 1) as e:
                            pick(e + 1)
                            scatter(e - 1)
                            gather(e + 1)
                else:
                    scatter(0)
                if NEXP > 2:
                    scatter(NEXP - 2)
                scatter(NEXP - 1)
                pool.wait_ge(added, 32 * NEXP)

            @block.tensor
            def _(pe):
                def make_list(e):
                    pe.wait_ge(oh_ready, TT * e + TT)
                    for t in range(TT):
                        pe.matmul(ps[:, 4, 320:326], OH[:, t, 0:P], RT[:, t, :], start=(t == 0), stop=(t == TT - 1))
                    for t in range(TT):
                        last = pe.matmul(ps[0:CAP2, 4, 328:334], OH[:, t, P:CAP], RT[:, t, :], start=(t == 0), stop=(t == TT - 1))
                    last.then_inc(ls_psum, 1)

                def turn_tokens(e):
                    pe.wait_ge(gathered, 32 * e + 32)
                    if not is_static(e, 0):
                        pe.wait_ge(xe_done, 2 * e)
                    for k in range(G):
                        at = (k % 2) * CAP
                        pe.transpose(ps[:, 4 + k // 2, at:at + P], XG[:, 0, k * P:(k + 1) * P], ident[:, :])
                        last = pe.transpose(ps[:, 4 + k // 2, at + P:at + CAP], XG[0:CAP2, 1, k * P:(k + 1) * P],
                                            ident[0:CAP2, 0:CAP2])
                    last.then_inc(xe_psum, 1)

                def up(u, j, tokens, cap, w):
                    n = J * u + j
                    if j % 2 == 0:
                        pe.wait_ge(ring_in[j // 2], 16 * (u + 1))
                    if not (isinstance(u, int) and n < 2):
                        pe.wait_ge(gu_done, n - 1)
                    for part in range(2):
                        for k in range(G):
                            last = pe.matmul(h_view(j, part, w), up_w(j, part, k), tokens(k),
                                             start=(k == 0 and (part == 0 or cap == HALF)), stop=(k == G - 1), skip_group_check=True)
                    last.then_inc(h_psum, 1)

                def down(u, j, w):
                    pe.wait_ge(gu_done, J * u + j + 1)
                    if j == 0 and not is_static(u, FIRST):
                        pe.wait_ge(ot_copied, 2 * (u - FIRST))
                    for g in range(G):
                        at = (g % 2) * CAP
                        last = pe.matmul(ps[:, g // 2, at:at + w], down_w(j)[:, g * P:(g + 1) * P], GU[:, j % 3, 0:w],
                                         start=(j == 0 and g % 2 == 0), stop=(j == J - 1), skip_group_check=True)
                    last.then_inc(dn_done, 1)

                def down_shared(u, j):
                    pe.wait_ge(gu_done, J * u + j + 1)
                    if j == 0 and u == 1:
                        pe.wait_ge(so_added, 4)
                    for t in range(4):
                        last = pe.matmul(ps[:, 4 + t, :], GU[:, j % 3, t * P:(t + 1) * P], down_w(j), start=(j == 0), stop=(j == J - 1))
                    last.then_inc(dn_done, 1)

                def turn_out(e):
                    pe.wait_ge(ot_copied, 2 * e + 2)
                    if not is_static(e, 0):
                        pe.wait_ge(y_ready, 2 * e)
                    for g in range(G):
                        pe.transpose(ps[:, 6, g * P:(g + 1) * P], OT[:, g, 0:P], ident[:, :])
                        last = pe.transpose(ps[0:CAP2, 7, g * P:(g + 1) * P], OT[:, g, P:CAP], ident[:, :])
                    last.then_inc(y_psum, 1)

                def products(e, w, last):
                    u = FIRST + e
                    pe.wait_ge(xe_done, 2 * e + 2)
                    for j in range(J):
                        up(u, j, lambda k: XE[:, k, 0:w], CAP, w)
                        if j == 0 and not is_static(e, 0):
                            turn_out(e - 1)
                        if j >= LAG:
                            down(u, j - LAG, w)
                        if j == 5 and not last:
                            make_list(e + 1)
                        if j == J - 2 and not last:
                            turn_tokens(e + 1)
                    for j in range(J - LAG, J):
                        down(u, j, w)

                def expert(e, last=False):
                    if is_static(e, 0):
                        products(e, CAP, last)
                        return
                    i = pe.value_load(width[0:1, bass.ds(e, 1)], min_val=0, max_val=3)

                    def choose(n):
                        if n == len(WIDTHS) - 1:
                            products(e, WIDTHS[n], last)
                            return
                        with pe.If(i < n + 1):
                            products(e, WIDTHS[n], last)
                        with pe.Else():
                            choose(n + 1)

                    choose(0)

                make_list(0)
                pe.wait_ge(list_ready, 2)
                for half in range(2):
                    cols = slice(half * HALF, half * HALF + HALF)
                    for j in range(J + LAG):
                        if j < J:
                            up(half, j, lambda k: XT[:, k, cols], HALF, HALF)
                        if j >= LAG:
                            down_shared(half, j - LAG)
                pe.wait_ge(so_added, 8)
                turn_tokens(0)
                expert(0)
                expert(1, NEXP == 2)
                if NEXP > 2:
                    if NEXP > 3:
                        with pe.Fori(2, NEXP - 1) as e:
                            expert(e)
                    expert(NEXP - 1, True)
                turn_out(NEXP - 1)


_OUT = (T + CAP, D)


def kernel(**inputs):
    import numpy as np
    import concourse.bacc as bacc
    from concourse.bass_utils import run_bass_kernel_spmd as run

    a = {k: np.asarray(v) for k, v in inputs.items()}
    c = np.ascontiguousarray

    def feature_major(w):
        return c(w.T.reshape(G, P, w.shape[0]).transpose(1, 0, 2))

    def chunks(w1, w2):
        n = w1.shape[0]
        all_ = np.empty((n, J, P, CW), w1.dtype)
        up = w1.reshape(n, 2, J, P, G, P)
        for part in range(2):
            v = all_[:, :, :, part * G * P:(part + 1) * G * P].reshape(n, J, P, G, P)
            v[...] = up[:, 1 - part].transpose(0, 1, 4, 3, 2)
        all_[:, :, :, 2 * G * P:] = w2.reshape(n, D, J, P).transpose(0, 2, 3, 1)
        return c(all_.reshape(n, PAIRS, 2, P, CW).transpose(0, 1, 3, 2, 4))

    ctx = a["ctx_1024"]
    named = {
        "x": c(a["x"]),
        "ctx_k": c(ctx.transpose(0, 2, 1).reshape(B, G, P, SK).transpose(0, 2, 1, 3)),
        "ctx_v": c(ctx),
        "wq": feature_major(a["L0_attn_wq_w"]), "wk": feature_major(a["L0_attn_wk_w"]),
        "wv": feature_major(a["L0_attn_wv_w"]), "wo": feature_major(a["L0_attn_wo_w"]),
        "bq": c(a["L0_attn_wq_b"].reshape(G, P).T), "bk": c(a["L0_attn_wk_b"].reshape(G, P).T),
        "bv": c(a["L0_attn_wv_b"].reshape(1, D)), "bo": c(a["L0_attn_wo_b"].reshape(1, D)),
        "wg": feature_major(a["L0_ffn_wg"]),
        "shared": chunks(a["L0_ffn_shared_w1"][None], a["L0_ffn_shared_w2"][None])[0],
        "experts": chunks(a["L0_ffn_expert_w1"], a["L0_ffn_expert_w2"]),
    }
    nc = bacc.Bacc("TRN2", target_bir_lowering=False, num_devices=1)
    args = [nc.dram_tensor(f"in_{k}", v.shape, mybir.dt.from_np(v.dtype), kind="ExternalInput").ap() for k, v in named.items()]
    out = nc.dram_tensor("out_rows", _OUT, F32, kind="ExternalOutput").ap()
    program(nc, *args, out)
    r = run(nc, [{f"in_{k}": v for k, v in named.items()}], core_ids=[0])
    return r.results[0]["out_rows"][0:T].reshape(B, SQ, D)
```

```python
from contextlib import ExitStack

import concourse.bass as bass
from concourse import mybir

F32 = mybir.dt.float32
F32R = mybir.dt.float32r
BF16 = mybir.dt.bfloat16
I32 = mybir.dt.int32
ALU = mybir.AluOpType
ACT = mybir.ActivationFunctionType
AX = mybir.AxisListType

P = 128
B = 32
SQ = 32
SK = 257
D = 512
G = D // P
DH = 32
T = B * SQ
TT = T // P
NE = 64
TOPK = 8
FFN = 1536
J = FFN // P
CAP = 160
CAP2 = CAP - P
UP = 2 * G * P
CW = UP + D
PAIRS = J // 2
LAG = 3
HALF = T // 2
SCALE = float(DH) ** -0.5
EPS = 1e-5
FEPS = 1.1920928955078125e-07
MASKED = -(2.0 ** 126)


class Tally:

    def __init__(self, eng, sem):
        self.eng, self.sem, self.n = eng, sem, 0

    def did(self, ins):
        ins.then_inc(self.sem, 1)
        self.n += 1

    def settle(self):
        self.eng.wait_ge(self.sem, self.n)

    def then(self, ins):
        self.did(ins)
        self.settle()


def tile_stats(dve, X, stats, mv, t, ready, n, stats_done):
    dve.wait_ge(ready, n)
    dve.bn_stats(stats[:, t, :], X[:, t, :]).then_inc(stats_done, 1)
    dve.wait_ge(stats_done, 2 * t + 1)
    dve.bn_aggr(mv[:, t, :], stats[:, t, :]).then_inc(stats_done, 1)


def layernorm(dve, X, XN, mv, small, done, std_ready, xn_ready):
    var, r, a = small[:, 0, :], small[:, 1, :], small[:, 2, :]
    done.then(dve.tensor_scalar(var, mv[:, :, 1], EPS, None, ALU.add))
    dve.wait_ge(std_ready, 1)
    done.then(dve.reciprocal(r, r))
    done.then(dve.tensor_tensor(a, r, r, ALU.mult))
    done.then(dve.tensor_tensor(a, a, var, ALU.mult))
    done.then(dve.tensor_scalar(a, a, -0.5, 1.5, ALU.mult, ALU.add))
    done.then(dve.tensor_tensor(r, r, a, ALU.mult))
    for t in range(TT):
        dve.tensor_scalar(XN[:, t, :], X[:, t, :], mv[:, t, 0:1], r[:, t:t + 1],
                          ALU.subtract, ALU.mult).then_inc(xn_ready, 1)


def transpose_tiles(pe, ps, XN, ident, xn_ready, xt_psum, xt_copied):
    for t in range(TT):
        pe.wait_ge(xn_ready, t + 1)
        if t >= 2:
            pe.wait_ge(xt_copied, t - 1)
        for g in range(G):
            last = pe.transpose(ps[:, t % 2, g * P:(g + 1) * P], XN[:, t, g * P:(g + 1) * P], ident[:, :])
        last.then_inc(xt_psum, 1)


def copy_tiles(act, ps, XT, small, ln_done, std_ready, xt_psum, xt_copied):
    act.wait_ge(ln_done, 1)
    act.activation(small[:, 1, :], small[:, 0, :], ACT.Sqrt).then_inc(std_ready, 1)
    for t in range(TT):
        act.wait_ge(xt_psum, t + 1)
        act.activation(XT[:, :, t * P:(t + 1) * P], ps[:, t % 2, :].rearrange("p (g n) -> p g n", g=G),
                       ACT.Copy).then_inc(xt_copied, 1)


def program(nc, x, ctx_k, ctx_v, wq, wk, wv, wo, bq, bk, bv, bo, wg, shared, experts, out, NEXP=NE):
    root = ExitStack()
    with root:
        def allocator(stack):
            def sb(name, shape, dt=F32):
                return stack.enter_context(nc.sbuf_tensor(name, shape, dt))
            return sb

        def sem(name):
            return root.enter_context(nc.semaphore(name))

        sb = allocator(root)
        ps = root.enter_context(nc.psum_tensor("ps", [P, 8, 512], F32))
        xn_dram = nc.dram_tensor("xn_scratch", [T, D], F32, kind="Internal").ap()

        X = sb("X", [P, TT, D])
        ident = sb("ident", [P, P])
        stats = sb("stats", [P, TT, 6])
        mv = sb("mv", [P, TT, 2])
        small = sb("small", [P, 3, TT])
        x_dram = x.rearrange("b s d -> (b s) d").rearrange("(t p) d -> p t d", p=P)
        out_tiles = out[0:T, :].rearrange("(t p) d -> p t d", p=P)

        weights = root.enter_context(ExitStack())
        sb = allocator(weights)
        W = sb("W", [P, 4, G, D])
        bqk = sb("bqk", [P, 2, G])
        bvo = sb("bvo", [P, 2, D])
        w_in = sem("w_in")

        with ExitStack() as st:
            sb = allocator(st)
            XN = sb("a_XN", [P, TT, D])
            XT = sb("a_XT", [P, G, T])
            Q = sb("a_Q", [P, 4, G, P])
            K = sb("a_K", [P, 4, G, SK])
            V = sb("a_V", [P, 4, 3, D])
            PR = sb("a_PR", [P, 2, G, SK])
            PTa = sb("a_PTa", [P, 2, 2, G, P])
            PTb = sb("a_PTb", [1, 2, G, P])
            AT = sb("a_AT", [P, G, T])
            mx = sb("a_mx", [P, 2, G])
            nm = sb("a_nm", [P, 2, G])
            sm = sb("a_sm", [P, 2, G])
            rs = sb("a_rs", [P, 2, G])

            x_in = [sem(f"a_x_in{i}") for i in range(4)]
            stats0 = sem("a_stats0")
            stats1 = sem("a_stats1")
            k_in = [sem(f"a_k_in{i}") for i in range(4)]
            v_in = [sem(f"a_v_in{i}") for i in range(4)]
            ln_done = sem("a_ln_done")
            std_ready = sem("a_std_ready")
            xn_ready = sem("a_xn_ready")
            xt_psum = sem("a_xt_psum")
            xt_copied = sem("a_xt_copied")
            made = sem("a_made")
            zeroed = sem("a_zeroed")
            ident_ready = sem("a_ident_ready")
            q_ready = sem("a_q_ready")
            s_done = sem("a_s_done")
            max_done = sem("a_max_done")
            nm_done = sem("a_nm_done")
            exp_done = sem("a_exp_done")
            rec_done = sem("a_rec_done")
            pr_ready = sem("a_pr_ready")
            t_done = sem("a_t_done")
            pt_ready = sem("a_pt_ready")
            pv_done = sem("a_pv_done")
            at_ready = sem("a_at_ready")
            back_psum = sem("a_back_psum")
            x1_ready = sem("a_x1_ready")

            block = st.enter_context(nc.Block())

            @block.sync
            def _(sp):
                for i in range(4):
                    sp.dma_start(X[:, 2 * i:2 * i + 2, :], x_dram[:, 2 * i:2 * i + 2, :]).then_inc(x_in[i], 16)

                def load(q, first):
                    for i in range(4):
                        b = 4 * q + i
                        if not first:
                            sp.wait_ge(s_done, b - 3)
                        sp.dma_start(K[:, i, :, :], ctx_k[b]).then_inc(k_in[i], 16)
                        if not first:
                            sp.wait_ge(pv_done, b - 3)
                        sp.dma_start(V[:, i, 0:2, :], ctx_v[b, 0:2 * P, :].rearrange("(k p) d -> p k d", p=P)).then_inc(v_in[i], 16)
                        sp.dma_start(V[0:1, i, 2, :], ctx_v[b, 2 * P:SK, :]).then_inc(v_in[i], 16)

                load(0, True)
                with sp.Fori(1, TT) as q:
                    load(q, False)
                for i, w in enumerate((wq, wk, wv, wo)):
                    sp.dma_start(W[:, i, :, :], w).then_inc(w_in, 16)
                for i, v in enumerate((bq, bk)):
                    sp.dma_start(bqk[:, i, :], v).then_inc(w_in, 16)
                for i, v in enumerate((bv, bo)):
                    sp.dma_start(bvo[:, i, :], v.to_broadcast([P, D])).then_inc(w_in, 16)

            @block.gpsimd
            def _(pool):
                pool.memset(ident[:, :], 0.0).then_inc(made, 1)
                pool.memset(Q[:, :, :, :], 0.0).then_inc(zeroed, 1)
                pool.wait_ge(made, 1)
                pool.affine_select(out=ident[:, :], in_=ident[:, :], compare_op=ALU.not_equal, fill=1.0, base=0,
                                   pattern=[[-1, P]], channel_multiplier=1).then_inc(ident_ready, 1)
                pool.wait_ge(zeroed, 1)

                def queries(q, first):
                    pool.wait_ge(xt_copied, q + 1)
                    for i in range(4):
                        b = 4 * q + i
                        if not first:
                            pool.wait_ge(s_done, b - 3)
                        for h in range(4):
                            r = slice(32 * h, 32 * h + 32)
                            pool.tensor_copy(Q[r, i, :, r], XT[r, :, bass.ds(P * q + SQ * i, SQ)]).then_inc(q_ready, 1)

                queries(0, True)
                with pool.Fori(1, TT) as q:
                    queries(q, False)

            @block.tensor
            def _(pe):
                pe.wait_ge(ident_ready, 1)
                transpose_tiles(pe, ps, XN, ident, xn_ready, xt_psum, xt_copied)
                pe.wait_ge(xt_copied, TT)

                def scores(b, i, q, first):
                    pe.wait_ge(q_ready, 4 * b + 4)
                    pe.wait_ge(k_in[i], 16 * q + 16)
                    if not (first and i == 0):
                        pe.wait_ge(exp_done, 4 * b)
                    for g in range(G):
                        last = pe.matmul(ps[:, g, 0:SK], Q[:, i, g, :], K[:, i, g, :], start=True, stop=True)
                    last.then_inc(s_done, 1)

                def turn(b, i):
                    pe.wait_ge(pr_ready, b + 1)
                    for g in range(G):
                        for k in range(2):
                            pe.transpose(ps[:, 4 + k, g * P:(g + 1) * P], PR[:, i % 2, g, k * P:(k + 1) * P], ident[:, :])
                        last = pe.transpose(ps[0:1, 6, g * P:(g + 1) * P], PR[:, i % 2, g, 2 * P:SK], ident[:, :])
                    last.then_inc(t_done, 1)

                def values(b, i, vcount):
                    pe.wait_ge(pt_ready, 2 * b + 2)
                    pe.wait_ge(v_in[i], vcount)
                    for g in range(G):
                        w = slice(g * P, (g + 1) * P)
                        for k in range(2):
                            pe.matmul(ps[:, 7, w], V[:, i, k, w], PTa[:, i % 2, k, g, :], start=(k == 0), stop=False)
                        last = pe.matmul(ps[:, 7, w], V[0:1, i, 2, w], PTb[0:1, i % 2, g, :], start=False, stop=True)
                    last.then_inc(pv_done, 1)

                def quad(q, first):
                    for i in range(4):
                        b = 4 * q + i
                        scores(b, i, q, first)
                        if not (first and i < 2):
                            if not (first and i < 3):
                                pe.wait_ge(at_ready, 4 * b - 8)
                            values(b - 2, (i - 2) % 4, 32 * q + 32 * (i >= 2))
                        if not (first and i < 1):
                            turn(b - 1, (i - 1) % 4)

                quad(0, True)
                with pe.Fori(1, TT) as q:
                    quad(q, False)
                pe.wait_ge(at_ready, 4 * (B - 2))
                values(B - 2, 2, 32 * TT)
                turn(B - 1, 3)
                pe.wait_ge(at_ready, 4 * (B - 1))
                values(B - 1, 3, 32 * TT)
                pe.wait_ge(at_ready, 4 * B)
                for t in range(TT):
                    if t >= 2:
                        pe.wait_ge(x1_ready, t - 1)
                    for g in range(G):
                        last = pe.transpose(ps[:, t % 2, g * P:(g + 1) * P], AT[:, g, t * P:(t + 1) * P], ident[:, :])
                    last.then_inc(back_psum, 1)

            @block.scalar
            def _(act):
                copy_tiles(act, ps, XT, small, ln_done, std_ready, xt_psum, xt_copied)

                def copy_pt(b, i):
                    act.wait_ge(t_done, b + 1)
                    act.activation(PTa[:, i % 2, :, :, :].rearrange("p k g n -> p (k g n)"),
                                   ps[:, 4:6, :].rearrange("p k n -> p (k n)"), ACT.Copy).then_inc(pt_ready, 1)
                    act.activation(PTb[0:1, i % 2, :, :].rearrange("p g n -> p (g n)"), ps[0:1, 6, :],
                                   ACT.Copy).then_inc(pt_ready, 1)

                def quad(q, first):
                    for i in range(4):
                        b = 4 * q + i
                        act.wait_ge(nm_done, b + 1)
                        if not (first and i < 2):
                            act.wait_ge(t_done, b - 1)
                        for g in range(G):
                            act.activation(PR[:, i % 2, g, :], ps[:, g, 0:SK], ACT.Exp, bias=nm[:, i % 2, g:g + 1],
                                           scale=SCALE, accum_out=sm[:, i % 2, g:g + 1]).then_inc(exp_done, 1)
                        if not (first and i < 1):
                            if not (first and i < 3):
                                act.wait_ge(pv_done, b - 2)
                            copy_pt(b - 1, (i - 1) % 4)

                quad(0, True)
                with act.Fori(1, TT) as q:
                    quad(q, False)
                act.wait_ge(pv_done, B - 2)
                copy_pt(B - 1, 3)

            @block.vector
            def _(dve):
                for t in range(TT):
                    tile_stats(dve, X, stats, mv, t, x_in[t // 2], 16, stats0)
                dve.wait_ge(stats0, 2 * TT)
                layernorm(dve, X, XN, mv, small, Tally(dve, ln_done), std_ready, xn_ready)

                def diagonal(b, q, i):
                    dve.wait_ge(pv_done, b + 1)
                    for h in range(4):
                        r = slice(32 * h, 32 * h + 32)
                        dve.tensor_copy(AT[r, :, bass.ds(P * q + SQ * i, SQ)],
                                        ps[r, 7, :].rearrange("p (g n) -> p g n", g=G)[:, :, r]).then_inc(at_ready, 1)

                def quad(q, first):
                    for i in range(4):
                        b = 4 * q + i
                        k = i % 2
                        dve.wait_ge(s_done, b + 1)
                        dve.tensor_reduce(mx[:, k, :], ps[:, 0:G, 0:SK], AX.X, ALU.max).then_inc(max_done, 1)
                        dve.wait_ge(max_done, b + 1)
                        if not (first and i < 2):
                            dve.wait_ge(exp_done, 4 * b - 4)
                        dve.tensor_scalar(nm[:, k, :], mx[:, k, :], -SCALE, None, ALU.mult).then_inc(nm_done, 1)
                        if not (first and i < 2):
                            if i < 2:
                                diagonal(b - 2, q - 1, i + 2)
                            else:
                                diagonal(b - 2, q, i - 2)
                        dve.wait_ge(exp_done, 4 * b + 4)
                        dve.reciprocal(rs[:, k, :], sm[:, k, :]).then_inc(rec_done, 1)
                        dve.wait_ge(rec_done, b + 1)
                        dve.tensor_tensor(PR[:, k, :, :], PR[:, k, :, :], rs[:, k, :].rearrange("p (g o) -> p g o", o=1).to_broadcast([P, G, SK]),
                                          ALU.mult).then_inc(pr_ready, 1)

                quad(0, True)
                with dve.Fori(1, TT) as q:
                    quad(q, False)
                diagonal(B - 2, TT - 1, 2)
                diagonal(B - 1, TT - 1, 3)
                for t in range(TT):
                    dve.wait_ge(back_psum, t + 1)
                    dve.tensor_tensor(X[:, t, :], X[:, t, :], ps[:, t % 2, :], ALU.add).then_inc(x1_ready, 1)
                    tile_stats(dve, X, stats, mv, t, x1_ready, t + 1, stats1)
                dve.wait_ge(stats1, 2 * TT)

        with ExitStack() as st:
            sb = allocator(st)
            XN = sb("b_XN", [P, TT, D])
            XT = sb("b_XT", [P, G, T])
            QT = sb("b_QT", [P, G, T])
            KT = sb("b_KT", [P, G, T])
            VV = sb("b_VV", [P, TT, D])
            Q = sb("b_Q", [P, 2, 4, G, P])
            mask = sb("b_mask", [1, 1, T], BF16)
            ones = sb("b_ones", [1, P], BF16)
            S = sb("b_S", [P, 3, 4 * G, SQ])
            PT = sb("b_PT", [P, 2, G, 4, P])
            AT = sb("b_AT", [P, G, T])
            mx = sb("b_mx", [P, 4 * G])
            sm = sb("b_sm", [P, 4 * G])

            ln_done = sem("b_ln_done")
            std_ready = sem("b_std_ready")
            xn_ready = sem("b_xn_ready")
            xt_psum = sem("b_xt_psum")
            xt_copied = sem("b_xt_copied")
            consts = sem("b_consts")
            mask_ready = sem("b_mask_ready")
            proj_psum = sem("b_proj_psum")
            proj_even = sem("b_proj_even")
            proj_odd = sem("b_proj_odd")
            v_copied = sem("b_v_copied")
            x_bias = sem("b_x_bias")
            q_ready = sem("b_q_ready")
            s_done = sem("b_s_done")
            soft = sem("b_soft")
            sub_done = sem("b_sub_done")
            exp_done = sem("b_exp_done")
            pr_ready = sem("b_pr_ready")
            t_done = sem("b_t_done")
            pt_ready = sem("b_pt_ready")
            pv_done = sem("b_pv_done")
            at_ready = sem("b_at_ready")
            o_psum = sem("b_o_psum")
            o_added = sem("b_o_added")
            stats2 = sem("b_stats2")

            block = st.enter_context(nc.Block())

            @block.gpsimd
            def _(pool):
                pool.memset(Q[:, :, :, :, :], 0.0).then_inc(consts, 1)
                pool.memset(PT[:, :, :, :, :], 0.0).then_inc(consts, 1)
                pool.memset(ones[:, :], 1.0).then_inc(consts, 1)

            @block.tensor
            def _(pe):
                transpose_tiles(pe, ps, XN, ident, xn_ready, xt_psum, xt_copied)
                pe.wait_ge(xt_copied, TT)
                pe.wait_ge(w_in, 16 * 8)
                n = 0

                def bank():
                    if n >= 20:
                        pe.wait_ge(v_copied, n - 19)
                    elif n >= 4:
                        pe.wait_ge(proj_even if n % 2 == 0 else proj_odd, (n - 4) // 2 + 1)
                    return ps[:, 2 + n % 4, :]

                for half in range(2):
                    cols = slice(half * HALF, half * HALF + HALF)
                    for o in range(G):
                        for i in range(2):
                            dst = bank()
                            for k in range(G):
                                last = pe.matmul(dst, W[:, i, k, o * P:(o + 1) * P], XT[:, k, cols], start=(k == 0), stop=(k == G - 1))
                            last.then_inc(proj_psum, 1)
                            n += 1
                def scores(t, g, b):
                    if g == 0 and b == 0:
                        pe.wait_ge(q_ready, 4 * t + 4)
                        if t >= 2:
                            pe.wait_ge(sub_done, t - 1)
                        pe.matmul(ps[:, t % 2, :], ones[:, :], mask[0:1, :, t * P:(t + 1) * P].to_broadcast([1, G, P]),
                                  start=True, stop=False, skip_group_check=True)
                    c = g * P + b * SQ
                    last = pe.matmul(ps[:, t % 2, c:c + SQ], Q[:, t % 2, b, g, :], KT[:, g, t * P + b * SQ:t * P + (b + 1) * SQ],
                                     start=False, stop=(g == 3 and b == 3), skip_group_check=True)
                    if g == 3 and b == 3:
                        last.then_inc(s_done, 1)

                def turn(t):
                    pe.wait_ge(pr_ready, t + 1)
                    if t >= 1:
                        pe.wait_ge(pt_ready, 4 * t)
                    for g in range(G):
                        last = pe.transpose(ps[:, 2, g * P:(g + 1) * P], S[:, t % 3, 4 * g:4 * g + 4, :].rearrange("p b n -> p (b n)"), ident[:, :])
                    last.then_inc(t_done, 1)

                def values(t, g):
                    if g == 0:
                        pe.wait_ge(pt_ready, 4 * t + 4)
                    if g % 2 == 0 and t >= 1:
                        pe.wait_ge(at_ready, 8 * t - 4 + 2 * g)
                    last = pe.matmul(ps[:, 4 + g, :], VV[:, t, g * P:(g + 1) * P], PT[:, t % 2, g, :, :].rearrange("p b n -> p (b n)"),
                                     start=True, stop=True)
                    if g % 2 == 1:
                        last.then_inc(pv_done, 1)

                EARLY = 3
                pe.wait_ge(consts, 3)
                pe.wait_ge(mask_ready, 1)
                for t in range(TT):
                    dst = bank()
                    for k in range(G):
                        last = pe.matmul(dst, XT[:, k, t * P:(t + 1) * P], W[:, 2, k, :], start=(k == 0), stop=(k == G - 1))
                        if k == G - 1:
                            last.then_inc(proj_psum, 1)
                        if 0 <= t - (TT - EARLY - 1) < EARLY:
                            for b in range(4):
                                scores(t - (TT - EARLY - 1), k, b)
                    n += 1
                pe.wait_ge(v_copied, 5)
                turn(0)
                pe.wait_ge(v_copied, TT)
                for t in range(EARLY, TT + 3):
                    for half in range(2):
                        for i in range(8 * half, 8 * half + 8):
                            if t < TT:
                                scores(t, i // 4, i % 4)
                            if i % 4 == 3:
                                values(t - 3, i // 4)
                        if half == 0 and t < TT + 2:
                            turn(t - 2)
                pe.wait_ge(at_ready, 8 * TT)
                for t in range(TT):
                    if t >= 2:
                        pe.wait_ge(o_added, t - 1)
                    for k in range(G):
                        last = pe.matmul(ps[:, t % 2, :], AT[:, k, t * P:(t + 1) * P], W[:, 3, k, :], start=(k == 0), stop=(k == G - 1))
                    last.then_inc(o_psum, 1)

            @block.scalar
            def _(act):
                copy_tiles(act, ps, XT, small, ln_done, std_ready, xt_psum, xt_copied)
                act.wait_ge(w_in, 16 * 8)
                n = 0
                for half in range(2):
                    for o in range(G):
                        act.wait_ge(proj_psum, n + 1)
                        act.activation(QT[:, o, half * HALF:half * HALF + HALF], ps[:, 2 + n % 4, :], ACT.Identity,
                                       bias=bqk[:, 0, o:o + 1]).then_inc(proj_even, 1)
                        n += 2

                def queries(t):
                    act.wait_ge(proj_even, 4 * (t // 4) + 4)
                    if t >= 2:
                        act.wait_ge(s_done, t - 1)
                    for h in range(4):
                        r = slice(32 * h, 32 * h + 32)
                        act.activation(Q[r, t % 2, :, :, r].rearrange("p b g n -> p g b n"),
                                       QT[r, :, t * P:(t + 1) * P].rearrange("p g (b n) -> p g b n", b=4), ACT.Copy).then_inc(q_ready, 1)

                act.wait_ge(consts, 3)
                queries(0)
                queries(1)
                def turned(t):
                    if t >= 2:
                        act.wait_ge(t_done, t - 1)
                        if t >= 4:
                            act.wait_ge(pv_done, 2 * t - 6)
                        for b in range(4):
                            r = slice(SQ * b, SQ * b + SQ)
                            act.activation(PT[r, t % 2, :, b, :], ps[r, 2, :].rearrange("p (g n) -> p g n", g=G), ACT.Copy).then_inc(pt_ready, 1)

                for t in range(TT + 2):
                    if t != 2:
                        turned(t)
                    if t < TT:
                        act.wait_ge(sub_done, t + 1)
                        act.activation(S[:, t % 3, :, :], S[:, t % 3, :, :], ACT.Exp, scale=SCALE).then_inc(exp_done, 1)
                    if t == 2:
                        turned(t)
                    if t + 2 < TT:
                        queries(t + 2)

            @block.vector
            def _(dve):
                layernorm(dve, X, XN, mv, small, Tally(dve, ln_done), std_ready, xn_ready)
                dve.wait_ge(xt_copied, TT)
                dve.tensor_scalar(mask[0:1, 0, :], XT[0:1, 0, :], 0.0, MASKED, ALU.is_equal, ALU.mult).then_inc(mask_ready, 1)
                dve.wait_ge(w_in, 16 * 8)
                n = 1
                for half in range(2):
                    for o in range(G):
                        dve.wait_ge(proj_psum, n + 1)
                        dve.tensor_scalar(KT[:, o, half * HALF:half * HALF + HALF], ps[:, 2 + n % 4, :], bqk[:, 1, o:o + 1], None,
                                          ALU.add).then_inc(proj_odd, 1)
                        n += 2
                chain = Tally(dve, soft)

                def take_v(t):
                    dve.wait_ge(proj_psum, 2 * TT + t + 1)
                    dve.tensor_tensor(VV[:, t, :], ps[:, 2 + t % 4, :], bvo[:, 0, :], ALU.add).then_inc(v_copied, 1)

                for t in range(3):
                    take_v(t)
                for t in range(TT):
                    dve.tensor_tensor(X[:, t, :], X[:, t, :], bvo[:, 1, :], ALU.add).then_inc(x_bias, 1)
                for t in range(3, TT - 3):
                    take_v(t)

                def diagonal(t, half):
                    dve.wait_ge(pv_done, 2 * t + half + 1)
                    for h in range(4):
                        r = slice(32 * h, 32 * h + 32)
                        g = slice(2 * half, 2 * half + 2)
                        dve.tensor_copy(AT[r, g, t * P:(t + 1) * P].rearrange("p g (b n) -> p g b n", b=4),
                                        ps[r, 4 + 2 * half:6 + 2 * half, :].rearrange("p g (b m) -> p g b m", b=4)[:, :, :, r]).then_inc(at_ready, 1)

                for t in range(TT + 3):
                    if t >= 3:
                        diagonal(t - 3, 0)
                    if t < TT:
                        dve.wait_ge(s_done, t + 1)
                        bk_ = ps[:, t % 2, :].rearrange("p (c n) -> p c n", n=SQ)
                        bc = lambda v: v[:, :].rearrange("p (c o) -> p c o", o=1).to_broadcast([P, 4 * G, SQ])
                        chain.then(dve.tensor_reduce(mx[:, :], bk_, AX.X, ALU.max))
                        if t >= 3:
                            dve.wait_ge(t_done, t - 2)
                        dve.tensor_tensor(S[:, t % 3, :, :], bk_, bc(mx), ALU.subtract).then_inc(sub_done, 1)
                    if t >= 3:
                        diagonal(t - 3, 1)
                    if t < TT:
                        dve.wait_ge(exp_done, t + 1)
                        chain.then(dve.tensor_reduce(sm[:, :], S[:, t % 3, :, :], AX.X, ALU.add))
                        chain.then(dve.reciprocal(sm[:, :], sm[:, :]))
                        dve.tensor_tensor(S[:, t % 3, :, :], S[:, t % 3, :, :], bc(sm), ALU.mult).then_inc(pr_ready, 1)
                        dve.wait_ge(pr_ready, t + 1)
                    if t < 3:
                        take_v(TT - 3 + t)
                dve.wait_ge(x_bias, TT)
                for t in range(TT):
                    dve.wait_ge(o_psum, t + 1)
                    dve.tensor_tensor(X[:, t, :], X[:, t, :], ps[:, t % 2, :], ALU.add).then_inc(o_added, 1)
                    tile_stats(dve, X, stats, mv, t, o_added, t + 1, stats2)
                dve.wait_ge(stats2, 2 * TT)

        weights.close()

        sb = allocator(root)
        RK = sb("RK", [P, NE, TT])
        WS = sb("WS", [P, NE, TT, 3], BF16)
        XSh = sb("XSh", [P, G, T], F32R)
        XSl = sb("XSl", [P, G, T], F32R)
        wide = sb("wide", [1, NE], I32)
        ring = sb("ring", [P, PAIRS, 2, CW])
        ring_in = [sem(f"ring_in{i}") for i in range(PAIRS)]
        with ExitStack() as st:
            sb = allocator(st)
            XN = sb("c_XN", [P, TT, D])
            XT = sb("c_XT", [P, G, T])
            wgs = sb("c_wg", [P, G, NE])
            L = sb("c_L", [P, TT, NE])
            M = sb("c_M", [P, TT, NE])
            sel = sb("c_sel", [P, TT, NE])
            selb = sb("c_selb", [P, TT, NE], BF16)
            before = sb("c_before", [P, P], BF16)
            ones = sb("c_ones", [P, P], BF16)
            top = sb("c_top", [P, TT, 8])
            red = sb("c_red", [P, 3, TT])
            zero = sb("c_zero", [P, D])

            wg_in = sem("c_wg_in")
            ln_done = sem("c_ln_done")
            std_ready = sem("c_std_ready")
            xn_ready = sem("c_xn_ready")
            xt_psum = sem("c_xt_psum")
            xt_copied = sem("c_xt_copied")
            consts = sem("c_consts")
            consts2 = sem("c_consts2")
            lg_psum = sem("c_lg_psum")
            shifted = sem("c_shifted")
            exped = sem("c_exped")
            chain_s = sem("c_chain")
            sel_ready = sem("c_sel_ready")
            rk_psum = sem("c_rk_psum")
            scratch_out = sem("c_scratch_out")
            xs_high = sem("c_xs_high")
            xs_low = sem("c_xs_low")

            block = st.enter_context(nc.Block())

            @block.sync
            def _(sp):
                sp.dma_start(wgs[:, :, :], wg).then_inc(wg_in, 16)
                for i in range(2):
                    sp.dma_start(ring[:, i, :, :], shared[i]).then_inc(ring_in[i], 16)
                sp.wait_ge(xn_ready, TT)
                sp.dma_start(xn_dram.rearrange("(t p) d -> p t d", p=P), XN[:, :, :]).then_inc(scratch_out, 16)
                sp.wait_ge(consts, 3)
                sp.dma_start(out[T:T + P, :], zero[:, :]).then_inc(scratch_out, 16)
                sp.dma_start(out[T + P:T + CAP, :], zero[0:CAP2, :]).then_inc(scratch_out, 16)
                for i in range(2, PAIRS):
                    sp.dma_start(ring[:, i, :, :], shared[i]).then_inc(ring_in[i], 16)
                sp.wait_ge(scratch_out, 48)

            @block.gpsimd
            def _(pool):
                pool.memset(before[:, :], 1.0).then_inc(consts, 1)
                pool.memset(ones[:, :], 1.0).then_inc(consts, 1)
                pool.memset(zero[:, :], 0.0).then_inc(consts, 1)
                pool.wait_ge(consts, 3)
                pool.affine_select(out=before[:, :], in_=before[:, :], compare_op=ALU.is_gt, fill=0.0, base=0,
                                   pattern=[[1, P]], channel_multiplier=-1).then_inc(consts2, 1)
                for k in range(G):
                    pool.wait_ge(xs_high, k + 1)
                    pool.tensor_tensor(XSl[:, k, :], XT[:, k, :], XSh[:, k, :], ALU.subtract).then_inc(xs_low, 1)
                pool.wait_ge(xs_low, G)

            @block.tensor
            def _(pe):
                transpose_tiles(pe, ps, XN, ident, xn_ready, xt_psum, xt_copied)
                pe.wait_ge(xt_copied, TT)
                pe.wait_ge(wg_in, 16)
                for t in range(TT):
                    for k in range(G):
                        last = pe.matmul(ps[:, 2, t * NE:(t + 1) * NE], XT[:, k, t * P:(t + 1) * P], wgs[:, k, :],
                                         start=(k == 0), stop=(k == G - 1))
                last.then_inc(lg_psum, 1)
                pe.wait_ge(consts2, 1)
                pe.wait_ge(sel_ready, 1)
                for t in range(TT):
                    for s in range(t + 1):
                        last = pe.matmul(ps[:, 3, t * NE:(t + 1) * NE], before[:, :] if s == t else ones[:, :], selb[:, s, :],
                                         start=(s == 0), stop=(s == t))
                for t in range(TT):
                    last = pe.matmul(ps[:, 4, 0:NE], ones[:, :], selb[:, t, :], start=(t == 0), stop=(t == TT - 1))
                last.then_inc(rk_psum, 1)

            @block.scalar
            def _(act):
                copy_tiles(act, ps, XT, small, ln_done, std_ready, xt_psum, xt_copied)
                act.wait_ge(xt_copied, TT)
                for k in range(G):
                    act.activation(XSh[:, k, :], XT[:, k, :], ACT.Copy).then_inc(xs_high, 1)
                act.wait_ge(shifted, 1)
                act.activation(L[:, :, :], L[:, :, :], ACT.Exp).then_inc(exped, 1)

            @block.vector
            def _(dve):
                layernorm(dve, X, XN, mv, small, Tally(dve, ln_done), std_ready, xn_ready)
                chain = Tally(dve, chain_s)
                bc = lambda v: v.rearrange("p (t o) -> p t o", o=1).to_broadcast([P, TT, NE])
                dve.wait_ge(lg_psum, 1)
                lg = ps[:, 2, :].rearrange("p (t e) -> p t e", e=NE)
                chain.then(dve.tensor_reduce(red[:, 0, :], lg, AX.X, ALU.max))
                dve.tensor_tensor(L[:, :, :], lg, bc(red[:, 0, :]), ALU.subtract).then_inc(shifted, 1)
                dve.wait_ge(exped, 1)
                chain.then(dve.tensor_reduce(red[:, 1, :], L[:, :, :], AX.X, ALU.add))
                chain.then(dve.reciprocal(red[:, 1, :], red[:, 1, :]))
                chain.then(dve.tensor_tensor(L[:, :, :], L[:, :, :], bc(red[:, 1, :]), ALU.mult))
                for t in range(TT):
                    chain.did(dve.max(top[:, t, :], L[:, t, :]))
                chain.settle()
                for t in range(TT):
                    chain.did(dve.match_replace(M[:, t, :], top[:, t, :], L[:, t, :], -1.0))
                chain.settle()
                chain.then(dve.tensor_scalar(sel[:, :, :], M[:, :, :], 0.0, None, ALU.is_lt))
                dve.tensor_copy(selb[:, :, :], sel[:, :, :]).then_inc(sel_ready, 1)
                chain.did(dve.tensor_reduce(red[:, 2, :], top[:, :, :], AX.X, ALU.add))
                chain.then(dve.tensor_tensor(L[:, :, :], L[:, :, :], sel[:, :, :], ALU.mult))
                chain.then(dve.tensor_scalar(red[:, 2, :], red[:, 2, :], FEPS, None, ALU.max))
                chain.then(dve.reciprocal(red[:, 2, :], red[:, 2, :]))
                chain.then(dve.tensor_tensor(L[:, :, :], L[:, :, :], bc(red[:, 2, :]), ALU.mult))
                for i in range(3):
                    part = WS[:, 0:NE, :, i].rearrange("p e t -> p t e")
                    chain.then(dve.tensor_copy(part, L[:, :, :]))
                    if i < 2:
                        chain.then(dve.tensor_tensor(L[:, :, :], L[:, :, :], part, ALU.subtract))
                dve.wait_ge(rk_psum, 1)
                rk = RK[:, 0:NE, :].rearrange("p e t -> p t e")
                chain.then(dve.scalar_tensor_tensor(rk, ps[:, 3, :].rearrange("p (t e) -> p t e", e=NE), 1.0, sel[:, :, :],
                                                    ALU.add, ALU.mult))
                chain.then(dve.tensor_scalar(RK[:, 0:NE, :], RK[:, 0:NE, :], -1.0, None, ALU.add))
                chain.then(dve.tensor_scalar(wide[:, :], ps[0:1, 4, 0:NE], float(P), None, ALU.is_gt))

        with ExitStack() as st:
            sb = allocator(st)
            SL = sb("d_SL", [P, 2, HALF])
            GF = sb("d_GF", [P, 2, HALF])
            GS = sb("d_GS", [P, 4, 2 * HALF], F32R)
            UPh = sb("d_UPh", [P, 2, UP], F32R)
            UPl = sb("d_UPl", [P, 2, UP], F32R)
            DNh = sb("d_DNh", [P, 4, D], F32R)
            DNl = sb("d_DNl", [P, 4, D], F32R)
            iota = sb("d_iota", [P, CAP], BF16)
            tick = sb("d_tick", [P, 1])
            RKe = sb("d_RKe", [P, TT])
            OH = sb("d_OH", [P, TT, CAP], BF16)
            RT = sb("d_RT", [P, TT, 6], BF16)
            LS = sb("d_LS", [P, 2, 6])
            slot = sb("d_slot", [P, 2])
            tk = sb("d_tk", [P, 4, 2])
            gidx = sb("d_gidx", [P, 2], I32)
            sidxn = sb("d_sidxn", [P, 2], I32)
            sidxh = sb("d_sidxh", [P, 2], I32)
            gateh = sb("d_gateh", [P, 2])
            sidx = sb("d_sidx", [P, 2], I32)
            gaten = sb("d_gaten", [P, 2])
            gate = sb("d_gate", [P, 2])
            XG = sb("d_XG", [P, 2, D])
            XE = sb("d_XE", [P, G, CAP])
            Y = sb("d_Y", [P, 2, D])
            YR = sb("d_YR", [CAP2, 2, D])

            h_psum = sem("d_h_psum")
            silu_done = sem("d_silu_done")
            gf_done = sem("d_gf_done")
            gh_done = sem("d_gh_done")
            gl_done = sem("d_gl_done")
            uph_done = sem("d_uph_done")
            upl_done = sem("d_upl_done")
            dnh_done = sem("d_dnh_done")
            dnl_done = sem("d_dnl_done")
            rest_s = sem("d_rest")
            dn_done = sem("d_dn_done")
            so_added = sem("d_so_added")
            so_out = sem("d_so_out")
            ls_clear = sem("d_ls_clear")
            consts = sem("d_consts")
            picked = sem("d_picked")
            ticked = sem("d_ticked")
            oh_ready = sem("d_oh_ready")
            ls_psum = sem("d_ls_psum")
            list_s = sem("d_list")
            list_ready = sem("d_list_ready")
            list_held = sem("d_list_held")
            list_kept = sem("d_list_kept")
            gathered = sem("d_gathered")
            xe_psum = sem("d_xe_psum")
            xe_done = sem("d_xe_done")
            y_ready = sem("d_y_ready")
            y2_ready = sem("d_y2_ready")
            added = sem("d_added")

            block = st.enter_context(nc.Block())

            FIRST = 2
            H_BANKS = (2, 3, 6)

            def up_w(j, part, k):
                at = (part * G + k) * P
                return ring[:, j // 2, j % 2, at:at + P]


            def gs(j, part, w):
                if w == HALF:
                    return GS[:, j % 4, part * HALF:(part + 1) * HALF]
                return GS[:, j % 4, 0:P] if part == 0 else GS[:, j % 4, CAP + CAP2:2 * CAP]

            def h_view(j, part, w):
                if w == HALF:
                    return ps[:, 2 * (j % 2) + part, :]
                return ps[:, H_BANKS[j % 3], part * CAP:part * CAP + w]

            def pair(bank):
                return ps[:, bank, 0:2 * CAP].rearrange("p (k n) -> p k n", k=2)

            def is_static(e, n):
                return isinstance(e, int) and e == n

            @block.sync
            def _(sp):
                def load(src, u, i):
                    sp.wait_ge(h_psum, J * (u - 1) + 2 * i + 2)
                    sp.wait_ge(dnl_done, J * (u - 1) + 2 * i + 2)
                    sp.dma_start(ring[:, i, :, :], src).then_inc(ring_in[i], 16)

                for i in range(PAIRS):
                    load(shared[i], 1, i)
                with sp.Fori(0, NEXP) as e:
                    for i in range(PAIRS):
                        load(experts[e, i], FIRST + e, i)

            @block.scalar
            def _(act):
                def silu(u, j, w):
                    n = J * u + j
                    act.wait_ge(h_psum, n + 1)
                    if not (isinstance(u, int) and n < 2):
                        act.wait_ge(gf_done, n - 1)
                    act.activation(SL[:, j % 2, 0:w], h_view(j, 0, w), ACT.Silu).then_inc(silu_done, 1)

                def high_up(n):
                    j = n % J
                    if j % 2 == 0:
                        act.wait_ge(ring_in[j // 2], 16 * (n // J + 1))
                    if n >= 2:
                        act.wait_ge(h_psum, n - 1)
                    act.activation(UPh[:, j % 2, :], ring[:, j // 2, j % 2, 0:UP], ACT.Copy).then_inc(uph_done, 1)

                def high_down(u, j):
                    n = J * u + j
                    if j % 2 == 0:
                        act.wait_ge(ring_in[j // 2], 16 * (u + 1))
                    if not (isinstance(u, int) and n < 4):
                        act.wait_ge(dn_done, n - 3)
                    act.activation(DNh[:, j % 4, :], ring[:, j // 2, j % 2, UP:CW], ACT.Copy).then_inc(dnh_done, 1)

                def high(u, j, w):
                    act.wait_ge(gf_done, J * u + j + 1)
                    act.activation(GS[:, j % 4, 0:w], GF[:, j % 2, 0:w], ACT.Copy).then_inc(gh_done, 1)

                def tokens(e):
                    act.wait_ge(xe_psum, e + 1)
                    if not is_static(e, 0):
                        act.wait_ge(h_psum, J * (FIRST + e))
                    for i in range(2):
                        act.activation(XE[:, 2 * i:2 * i + 2, :], pair(i if is_static(e, 0) else 4 + i), ACT.Copy).then_inc(xe_done, 1)

                def weigh(e):
                    act.wait_ge(dn_done, J * (FIRST + e) + J)
                    act.wait_ge(list_kept, 2 * e + 2)
                    if not is_static(e, 0):
                        act.wait_ge(added, 32 * e)
                    act.activation(Y[:, 0, :], ps[:, 0, :], ACT.Copy, scale=gate[:, 0:1]).then_inc(y_ready, 1)

                def expert(e, last=False):
                    for j in range(J):
                        silu(FIRST + e, j, CAP)
                        high_down(FIRST + e, j)
                        high(FIRST + e, j, CAP)
                        if j == J - 1 and not last:
                            tokens(e + 1)
                        if j == 0 and not is_static(e, 0):
                            weigh(e - 1)

                high_up(0)
                for half in range(2):
                    for j in range(J):
                        if J * half + j + 1 < 2 * J:
                            high_up(J * half + j + 1)
                        silu(half, j, HALF)
                        high_down(half, j)
                        high(half, j, HALF)
                tokens(0)
                expert(0)
                expert(1, NEXP == 2)
                if NEXP > 2:
                    if NEXP > 3:
                        with act.Fori(2, NEXP - 1) as e:
                            expert(e)
                    expert(NEXP - 1, True)
                weigh(NEXP - 1)

            @block.vector
            def _(dve):
                def product(u, j, w):
                    n = J * u + j
                    dve.wait_ge(silu_done, n + 1)
                    if not (isinstance(u, int) and n < 2):
                        dve.wait_ge(gh_done, n - 1)
                        dve.wait_ge(gl_done, n - 1)
                    dve.tensor_tensor(GF[:, j % 2, 0:w], SL[:, j % 2, 0:w], h_view(j, 1, w), ALU.mult).then_inc(gf_done, 1)

                def low_up(n):
                    j = n % J
                    dve.wait_ge(uph_done, n + 1)
                    dve.tensor_tensor(UPl[:, j % 2, :], ring[:, j // 2, j % 2, 0:UP], UPh[:, j % 2, :], ALU.subtract).then_inc(upl_done, 1)

                def low_down(u, j):
                    dve.wait_ge(dnh_done, J * u + j + 1)
                    dve.tensor_tensor(DNl[:, j % 4, :], ring[:, j // 2, j % 2, UP:CW], DNh[:, j % 4, :], ALU.subtract).then_inc(dnl_done, 1)

                def low(u, j, w):
                    dve.wait_ge(gh_done, J * u + j + 1)
                    if w == HALF:
                        dve.tensor_tensor(gs(j, 1, HALF), GF[:, j % 2, :], gs(j, 0, HALF), ALU.subtract).then_inc(gl_done, 1)
                        return
                    dve.tensor_tensor(gs(j, 1, P), GF[:, j % 2, 0:P], gs(j, 0, P), ALU.subtract)
                    dve.tensor_tensor(GS[:, j % 4, CAP:CAP + CAP2], GF[:, j % 2, P:CAP], GS[:, j % 4, P:CAP], ALU.subtract).then_inc(gl_done, 1)

                rest = Tally(dve, rest_s)

                def second_tile(e, step):
                    rest.n = 2 * e + step
                    if step == 0:
                        dve.wait_ge(dn_done, J * (FIRST + e) + J)
                        if not is_static(e, 0):
                            dve.wait_ge(y2_ready, e)
                        rest.did(dve.tensor_copy(YR[:, 0, :], ps[CAP2:2 * CAP2, 1, :]))
                    elif step == 1:
                        rest.settle()
                        rest.did(dve.tensor_tensor(YR[:, 1, :], YR[:, 0, :], ps[0:CAP2, 1, :], ALU.add))
                    else:
                        rest.settle()
                        if not is_static(e, 0):
                            dve.wait_ge(added, 32 * e)
                        dve.tensor_scalar(Y[0:CAP2, 1, :], YR[:, 1, :], gate[0:CAP2, 1:2], None, ALU.mult).then_inc(y2_ready, 1)

                def onehot(e, tiles):
                    dve.wait_ge(picked, 2 * e + 2)
                    for t in tiles:
                        dve.tensor_scalar(OH[:, t, :], iota[:, :], RKe[:, t:t + 1], None, ALU.is_equal).then_inc(oh_ready, 1)

                lists = Tally(dve, list_s)
                LIST_STEPS = 7

                def read_list(e):
                    lists.n = LIST_STEPS * e
                    dve.wait_ge(ls_psum, e + 1)
                    lists.did(dve.tensor_copy(LS[:, 0, :], ps[:, 4, 320:326]))
                    lists.did(dve.tensor_copy(LS[0:CAP2, 1, :], ps[0:CAP2, 4, 328:334]))
                    lists.settle()
                    token, a = tk[:, 0, :], tk[:, 1, :]
                    lists.did(dve.tensor_reduce(token, LS[:, :, 0:2], AX.X, ALU.add))
                    lists.did(dve.tensor_reduce(gaten[:, :], LS[:, :, 3:6], AX.X, ALU.add))
                    lists.then(dve.tensor_tensor(a, LS[:, :, 2], slot[:, :], ALU.mult))
                    lists.then(dve.tensor_tensor(a, a, token, ALU.subtract))
                    lists.then(dve.tensor_tensor(a, slot[:, :], a, ALU.subtract))
                    if not is_static(e, 0):
                        dve.wait_ge(gathered, 32 * e)
                    if not is_static(e, 0):
                        dve.wait_ge(list_held, 2 * e)
                    dve.tensor_copy(sidxn[:, :], a).then_inc(list_ready, 1)
                    dve.tensor_copy(gidx[:, :], token).then_inc(list_ready, 1)
                    dve.wait_ge(list_ready, 2 * e + 2)

                def hold_list(e):
                    if not is_static(e, 0):
                        dve.wait_ge(list_kept, 2 * e)
                    dve.tensor_copy(sidxh[:, :], sidxn[:, :]).then_inc(list_held, 1)
                    dve.tensor_copy(gateh[:, :], gaten[:, :]).then_inc(list_held, 1)

                def keep_list(e):
                    if not is_static(e, 0):
                        dve.wait_ge(added, 32 * e)
                        dve.wait_ge(y_ready, e)
                        dve.wait_ge(y2_ready, e)
                    dve.wait_ge(list_held, 2 * e + 2)
                    dve.tensor_copy(sidx[:, :], sidxh[:, :]).then_inc(list_kept, 1)
                    dve.tensor_copy(gate[:, :], gateh[:, :]).then_inc(list_kept, 1)
                    dve.wait_ge(list_kept, 2 * e + 2)

                def expert(e, last=False):
                    for j in range(J):
                        product(FIRST + e, j, CAP)
                        low_down(FIRST + e, j)
                        low(FIRST + e, j, CAP)
                        if j < 3 and not is_static(e, 0):
                            second_tile(e - 1, j)
                        if j in (3, 4) and not last:
                            onehot(e + 1, range(4 * (j - 3), 4 * (j - 2)))
                        if j == 5 and not last:
                            if not is_static(e, 0):
                                hold_list(e)
                            read_list(e + 1)
                        if j == 7 and not is_static(e, 0):
                            if last:
                                hold_list(e)
                            keep_list(e)

                low_up(0)
                low_up(1)
                dve.memset(LS[:, :, :], 0.0).then_inc(ls_clear, 1)
                dve.wait_ge(ls_clear, 1)
                dve.wait_ge(consts, 5)
                onehot(0, range(TT))
                for half in range(2):
                    for j in range(J):
                        if 1 < J * half + j + 1 < 2 * J:
                            low_up(J * half + j + 1)
                        if half == 0 and j == 1:
                            read_list(0)
                            hold_list(0)
                            keep_list(0)
                        product(half, j, HALF)
                        low_down(half, j)
                        low(half, j, HALF)
                    dve.wait_ge(dn_done, J * half + J)
                    for t in range(4):
                        row = 4 * half + t
                        dve.tensor_tensor(X[:, row, :], X[:, row, :], ps[:, 4 + t, :], ALU.add).then_inc(so_added, 1)
                expert(0)
                expert(1, NEXP == 2)
                if NEXP > 2:
                    if NEXP > 3:
                        with dve.Fori(2, NEXP - 1) as e:
                            expert(e)
                    expert(NEXP - 1, True)
                for step in range(3):
                    second_tile(NEXP - 1, step)

            @block.gpsimd
            def _(pool):
                exact = dict(allow_small_or_imprecise_dtypes=True)
                pool.iota(iota[:, :], [[1, CAP]], base=0, channel_multiplier=0, **exact).then_inc(consts, 1)
                pool.iota(slot[:, :], [[P, 2]], base=T, channel_multiplier=1, **exact).then_inc(consts, 1)
                pool.iota(RT[:, :, 0], [[P, TT]], base=0, channel_multiplier=0, **exact).then_inc(consts, 1)
                pool.iota(RT[:, :, 1], [[0, TT]], base=0, channel_multiplier=1, **exact).then_inc(consts, 1)
                pool.memset(RT[:, :, 2], 1.0).then_inc(consts, 1)
                pool.wait_ge(consts, 5)

                def pick(e):
                    if not (isinstance(e, int) and e == 0):
                        pool.wait_ge(ls_psum, e)
                    pool.tensor_copy(RKe[:, :], RK[:, bass.ds(e, 1), :].rearrange("p o t -> p (o t)")).then_inc(picked, 1)
                    pool.tensor_copy(RT[:, :, 3:6], WS[:, bass.ds(e, 1), :, :].rearrange("p o t c -> p (o t) c")).then_inc(picked, 1)

                def hold(before):
                    if not (isinstance(before, int) and before == 0):
                        pool.wait_ge(ticked, before)
                    pool.tensor_tensor(tick[:, :], iota[:, 0:1], iota[:, 0:1], ALU.add).then_inc(ticked, 1)

                def gather(e):
                    pool.wait_ge(list_ready, 2 * e + 2)
                    if not (isinstance(e, int) and e == 0):
                        pool.wait_ge(xe_psum, e)
                    hold(e if isinstance(e, int) and e < 2 else 2 * e - 1)
                    pool.indirect_dma_start(XG[:, 0, :], None, xn_dram, bass.IndirectOffsetOnAxis(gidx[:, 0:1], 0)).then_inc(gathered, 16)
                    pool.indirect_dma_start(XG[0:CAP2, 1, :], None, xn_dram, bass.IndirectOffsetOnAxis(gidx[0:CAP2, 1:2], 0)).then_inc(gathered, 16)

                def scatter(e):
                    pool.wait_ge(y_ready, e + 1)
                    pool.wait_ge(y2_ready, e + 1)
                    if not (isinstance(e, int) and e == 0):
                        pool.wait_ge(added, 32 * e)
                    hold(2 * e + 1 if isinstance(e, int) and e == NEXP - 1 else 2 * e + 2)
                    pool.indirect_dma_start(out, bass.IndirectOffsetOnAxis(sidx[:, 0:1], 0), Y[:, 0, :], None,
                                            compute_op=ALU.add).then_inc(added, 16)
                    pool.indirect_dma_start(out, bass.IndirectOffsetOnAxis(sidx[0:CAP2, 1:2], 0), Y[0:CAP2, 1, :], None,
                                            compute_op=ALU.add).then_inc(added, 16)

                pick(0)
                gather(0)
                pick(1)
                for half in range(2):
                    pool.wait_ge(so_added, 4 * half + 4)
                    pool.dma_start(out_tiles[:, 4 * half:4 * half + 4, :], X[:, 4 * half:4 * half + 4, :]).then_inc(so_out, 16)
                pool.wait_ge(so_out, 32)
                gather(1)
                if NEXP > 2:
                    pick(2)
                    scatter(0)
                    gather(2)
                    if NEXP > 3:
                        with pool.Fori(2, NEXP - 1) as e:
                            pick(e + 1)
                            scatter(e - 1)
                            gather(e + 1)
                else:
                    scatter(0)
                if NEXP > 2:
                    scatter(NEXP - 2)
                scatter(NEXP - 1)
                pool.wait_ge(added, 32 * NEXP)

            @block.tensor
            def _(pe):
                def make_list(e):
                    pe.wait_ge(oh_ready, TT * e + TT)
                    for t in range(TT):
                        pe.matmul(ps[:, 4, 320:326], OH[:, t, 0:P], RT[:, t, :], start=(t == 0), stop=(t == TT - 1))
                    for t in range(TT):
                        last = pe.matmul(ps[0:CAP2, 4, 328:334], OH[:, t, P:CAP], RT[:, t, :], start=(t == 0), stop=(t == TT - 1))
                    last.then_inc(ls_psum, 1)

                def turn_tokens(e):
                    first = 0 if is_static(e, 0) else 4
                    pe.wait_ge(gathered, 32 * e + 32)
                    if not is_static(e, 0):
                        pe.wait_ge(xe_done, 2 * e)
                    for k in range(G):
                        at = (k % 2) * CAP
                        pe.transpose(ps[:, first + k // 2, at:at + P], XG[:, 0, k * P:(k + 1) * P], ident[:, :])
                        last = pe.transpose(ps[:, first + k // 2, at + P:at + CAP], XG[0:CAP2, 1, k * P:(k + 1) * P],
                                            ident[0:CAP2, 0:CAP2])
                    last.then_inc(xe_psum, 1)

                def parts(dst, terms, start, stop):
                    for i, (kept, streamed) in enumerate(terms):
                        last = pe.matmul(dst, kept, streamed, start=start and i == 0, stop=stop and i == len(terms) - 1,
                                         skip_group_check=True)
                    return last

                def up_shared(u, j, cols):
                    n = J * u + j
                    pe.wait_ge(upl_done, n + 1)
                    if n >= 2:
                        pe.wait_ge(gf_done, n - 1)
                    for part in range(2):
                        for k in range(G):
                            at = slice((part * G + k) * P, (part * G + k + 1) * P)
                            h, l = UPh[:, j % 2, at], UPl[:, j % 2, at]
                            last = parts(h_view(j, part, HALF), ((h, XSh[:, k, cols]), (h, XSl[:, k, cols]), (l, XSh[:, k, cols])),
                                         k == 0, k == G - 1)
                    last.then_inc(h_psum, 1)

                def up(e, j, w):
                    u = FIRST + e
                    n = J * u + j
                    if j % 2 == 0:
                        pe.wait_ge(ring_in[j // 2], 16 * (u + 1))
                    if is_static(e, 0) and j == 2:
                        pe.wait_ge(so_added, 8)
                    if j >= 3:
                        pe.wait_ge(gf_done, n - 2)
                    for part in range(2):
                        for k in range(G):
                            last = pe.matmul(h_view(j, part, w), up_w(j, part, k), XE[:, k, 0:w],
                                             start=(k == 0 and part == 0), stop=(k == G - 1), skip_group_check=True)
                    last.then_inc(h_psum, 1)

                def down(e, j, w):
                    pe.wait_ge(gl_done, J * (FIRST + e) + j + 1)
                    if j == 0 and not is_static(e, 0):
                        pe.wait_ge(y_ready, e)
                        pe.wait_ge(rest_s, 2 * e)
                    h, l = DNh[:, j % 4, :], DNl[:, j % 4, :]
                    gh, gl = gs(j, 0, P), gs(j, 1, P)
                    last = parts(ps[:, 0, :], ((gh, h), (gh, l), (gl, h)), j == 0, j == J - 1)
                    if w == CAP:
                        pe.matmul(ps[0:2 * CAP2, 1, :], GS[:, j % 4, P:P + 2 * CAP2], h, start=(j == 0), stop=False, skip_group_check=True)
                        last = pe.matmul(ps[0:CAP2, 1, :], GS[:, j % 4, P:CAP], l, start=False, stop=(j == J - 1), skip_group_check=True)
                    last.then_inc(dn_done, 1)

                def down_shared(u, j):
                    pe.wait_ge(gl_done, J * u + j + 1)
                    if j == 0 and u == 1:
                        pe.wait_ge(so_added, 4)
                    h, l = DNh[:, j % 4, :], DNl[:, j % 4, :]
                    for t in range(4):
                        rows = slice(t * P, (t + 1) * P)
                        gh, gl = gs(j, 0, HALF)[:, rows], gs(j, 1, HALF)[:, rows]
                        last = parts(ps[:, 4 + t, :], ((gh, h), (gh, l), (gl, h)), j == 0, j == J - 1)
                    last.then_inc(dn_done, 1)

                def products(e, w, last):
                    pe.wait_ge(xe_done, 2 * e + 2)
                    for j in range(J):
                        up(e, j, w)
                        if j == J - 1 and not last:
                            turn_tokens(e + 1)
                        if j >= LAG:
                            down(e, j - LAG, w)
                        if j == 5 and not last:
                            make_list(e + 1)
                    for j in range(J - LAG, J):
                        down(e, j, w)

                def expert(e, last=False):
                    if is_static(e, 0):
                        products(e, CAP, last)
                        return
                    i = pe.value_load(wide[0:1, bass.ds(e, 1)], min_val=0, max_val=1)
                    with pe.If(i < 1):
                        products(e, P, last)
                    with pe.Else():
                        products(e, CAP, last)

                for half in range(2):
                    cols = slice(half * HALF, half * HALF + HALF)
                    for j in range(J + LAG):
                        if j < J:
                            up_shared(half, j, cols)
                        if half == 0 and j == 1:
                            make_list(0)
                        if half == 0 and j == LAG:
                            pe.wait_ge(list_ready, 2)
                        if half == 1 and j == J + 1:
                            pe.wait_ge(gf_done, 2 * J)
                            turn_tokens(0)
                        if j >= LAG:
                            down_shared(half, j - LAG)
                expert(0)
                expert(1, NEXP == 2)
                if NEXP > 2:
                    pairs = (NEXP - 3) // 2
                    if pairs:
                        with pe.Fori(0, pairs) as i:
                            expert(2 * i + 2)
                            expert(2 * i + 3)
                    for e in range(2 + 2 * pairs, NEXP):
                        expert(e, e == NEXP - 1)


_OUT = (T + CAP, D)


def kernel(**inputs):
    import numpy as np
    import concourse.bacc as bacc
    from concourse.bass_utils import run_bass_kernel_spmd as run

    a = {k: np.asarray(v) for k, v in inputs.items()}
    c = np.ascontiguousarray

    def feature_major(w):
        return c(w.T.reshape(G, P, w.shape[0]).transpose(1, 0, 2))

    def chunks(w1, w2):
        n = w1.shape[0]
        all_ = np.empty((n, J, P, CW), w1.dtype)
        up = w1.reshape(n, 2, J, P, G, P)
        for part in range(2):
            v = all_[:, :, :, part * G * P:(part + 1) * G * P].reshape(n, J, P, G, P)
            v[...] = up[:, 1 - part].transpose(0, 1, 4, 3, 2)
        all_[:, :, :, UP:] = w2.reshape(n, D, J, P).transpose(0, 2, 3, 1)
        return c(all_.reshape(n, PAIRS, 2, P, CW).transpose(0, 1, 3, 2, 4))

    ctx = a["ctx_1024"]
    named = {
        "x": c(a["x"]),
        "ctx_k": c(ctx.transpose(0, 2, 1).reshape(B, G, P, SK).transpose(0, 2, 1, 3)),
        "ctx_v": c(ctx),
        "wq": feature_major(a["L0_attn_wq_w"]), "wk": feature_major(a["L0_attn_wk_w"]),
        "wv": feature_major(a["L0_attn_wv_w"]), "wo": feature_major(a["L0_attn_wo_w"]),
        "bq": c(a["L0_attn_wq_b"].reshape(G, P).T), "bk": c(a["L0_attn_wk_b"].reshape(G, P).T),
        "bv": c(a["L0_attn_wv_b"].reshape(1, D)), "bo": c(a["L0_attn_wo_b"].reshape(1, D)),
        "wg": feature_major(a["L0_ffn_wg"]),
        "shared": chunks(a["L0_ffn_shared_w1"][None], a["L0_ffn_shared_w2"][None])[0],
        "experts": chunks(a["L0_ffn_expert_w1"], a["L0_ffn_expert_w2"]),
    }
    nc = bacc.Bacc("TRN2", target_bir_lowering=False, num_devices=1)
    args = [nc.dram_tensor(f"in_{k}", v.shape, mybir.dt.from_np(v.dtype), kind="ExternalInput").ap() for k, v in named.items()]
    out = nc.dram_tensor("out_rows", _OUT, F32, kind="ExternalOutput").ap()
    program(nc, *args, out)
    r = run(nc, [{f"in_{k}": v for k, v in named.items()}], core_ids=[0])
    return r.results[0]["out_rows"][0:T].reshape(B, SQ, D)
```
